# Optimizing a Trainium2 kernel written in Bass

```python
import numpy as np
import jax
import jax.numpy as jnp

def _softmax(x, axis=-1):
    return jax.nn.softmax(x, axis=axis)

def _gelu(x):
    return jax.nn.gelu(x, approximate=True)

def _silu(x):
    return jax.nn.silu(x)

def _sigmoid(x):
    return jax.nn.sigmoid(x)

def _layernorm(x, axis=-1, eps=1e-05):
    m = jnp.mean(x, axis=axis, keepdims=True)
    v = jnp.var(x, axis=axis, keepdims=True)
    return (x - m) / jnp.sqrt(v + eps)

def _scatter_add(tgt, idx, src, axis=0):
    return tgt.at[idx].add(src)

def _segment_sum(src, seg, n):
    return jax.ops.segment_sum(src, seg, n)
kernel_name = 'mk_xattn_ffn_d1_seqx_r8_6e47cb'

def setup_inputs(seed: int=0):
    np.random.seed(seed)
    _w = jnp.asarray

    def _rec_inputs():
        import jax
        import jax.numpy as jnp
        _rk = jax.random.key(seed)
        x = -0.0005207 + 1.001 * jax.random.normal(jax.random.fold_in(_rk, 1), (4, 256, 128), jnp.float32)
        _lenS = 256 - jax.random.randint(jax.random.fold_in(_rk, 7), (4,), 0, max(1, 256 // 4) + 1, jnp.int32)
        _lenS2 = 512 - jax.random.randint(jax.random.fold_in(_rk, 8), (4,), 0, max(1, 512 // 4) + 1, jnp.int32)
        _ctx_1024P = jax.random.normal(jax.random.fold_in(_rk, 11), (4, 16, 128), jnp.float32)
        _ctx_1024c = jax.random.dirichlet(jax.random.fold_in(_rk, 511), 0.3 * jnp.ones((16,), jnp.float32), (4, 512))
        _ctx_1024t = jnp.einsum('bsk,bkd->bsd', _ctx_1024c, _ctx_1024P)
        _ctx_1024t = _ctx_1024t * jax.lax.rsqrt(jnp.mean(jnp.square(_ctx_1024t)) + 1e-12) * 0.953939
        ctx_1024 = -1.52775e-05 + 0.999936 * (_ctx_1024t + 0.3 * jax.random.normal(jax.random.fold_in(_rk, 611), (4, 512, 128), jnp.float32))
        return (x, ctx_1024)
    x, ctx_1024 = _rec_inputs()

    def _L0_xattn_setup():
        import jax, jax.numpy as jnp
        import numpy as np
        DIM = 128
        HEADS = 16
        DHEAD = 64
        INNER = HEADS * DHEAD
        EPS = 1e-05

        def layer_norm(x, g, b):
            mu = jnp.mean(x, axis=-1, keepdims=True)
            var = jnp.mean(jnp.square(x - mu), axis=-1, keepdims=True)
            return (x - mu) * jax.lax.rsqrt(var + EPS) * g + b

        def apply_rope(x, cos, sin):
            d2 = x.shape[-1] // 2
            x1, x2 = (x[..., :d2], x[..., d2:])
            return jnp.concatenate([x1 * cos - x2 * sin, x2 * cos + x1 * sin], axis=-1)
        key = jax.random.key(seed)
        ks = jax.random.split(key, 10)
        B, N, S = (8, 32, 512)
        latents = jax.random.normal(ks[0], (B, N, DIM), dtype=jnp.float32)
        context = jax.random.normal(ks[1], (B, S, DIM), dtype=jnp.float32)
        cos = jax.random.uniform(ks[2], (S, DHEAD // 2), dtype=jnp.float32)
        sin = jax.random.uniform(ks[3], (S, DHEAD // 2), dtype=jnp.float32)
        init = lambda k, shp, fan_in: jax.random.normal(k, shp, dtype=jnp.float32) / np.sqrt(fan_in)
        return {'latents': latents, 'context': context, 'cos': cos, 'sin': sin, 'ln_lat_g': jnp.ones((DIM,), jnp.float32), 'ln_lat_b': jnp.zeros((DIM,), jnp.float32), 'ln_ctx_g': jnp.ones((DIM,), jnp.float32), 'ln_ctx_b': jnp.zeros((DIM,), jnp.float32), 'Wq': init(ks[4], (DIM, INNER), DIM), 'Wkv': init(ks[5], (DIM, 2 * INNER), DIM), 'Wo': init(ks[6], (INNER, DIM), INNER), 'bo': jnp.zeros((DIM,), jnp.float32)}
    _L0_xattn_all = _L0_xattn_setup()
    _L0_xattn_in = {k: v for k, v in _L0_xattn_all.items() if k in ('cos', 'sin', 'ln_lat_g', 'ln_lat_b', 'ln_ctx_g', 'ln_ctx_b', 'Wq', 'Wkv', 'Wo', 'bo')}
    del _L0_xattn_all

    def _L0_ffn_setup():
        import jax, jax.numpy as jnp
        import numpy as np
        D = 128
        H = 16
        HD = D // H
        L = 64
        E = 8
        B, T = (4, 256)
        EPS = 1e-06

        def _glorot(k, shape):
            fan_in, fan_out = (shape[-2], shape[-1])
            lim = np.sqrt(6.0 / (fan_in + fan_out)).astype(np.float32)
            return jax.random.uniform(k, shape, jnp.float32, -lim, lim)

        def _rmsnorm(x, gamma):
            return gamma * x * jax.lax.rsqrt(jnp.mean(x * x, axis=-1, keepdims=True) + EPS)
        key = jax.random.key(seed)
        ks = jax.random.split(key, 8)
        return {'x': jax.random.normal(ks[0], (B, T, D), jnp.float32), 'gamma1': jnp.ones((D,), jnp.float32), 'Wq': _glorot(ks[1], (D, D)), 'bq': jnp.zeros((D,), jnp.float32), 'Wdown': _glorot(ks[2], (D, L)), 'bdown': jnp.zeros((L,), jnp.float32), 'Wup': _glorot(ks[3], (L, 2 * D)), 'bup': jnp.zeros((2 * D,), jnp.float32), 'Wo': _glorot(ks[4], (D, D)), 'bo': jnp.zeros((D,), jnp.float32), 'gamma2': jnp.ones((D,), jnp.float32), 'Wg': _glorot(ks[5], (D, E)), 'bg': jnp.zeros((E,), jnp.float32), 'We': _glorot(ks[6], (E, D, D))}
    _L0_ffn_all = _L0_ffn_setup()
    _L0_ffn_in = {k: v for k, v in _L0_ffn_all.items() if k in ('gamma1', 'Wq', 'bq', 'Wdown', 'bdown', 'Wup', 'bup', 'Wo', 'bo', 'gamma2', 'Wg', 'bg', 'We')}
    del _L0_ffn_all
    return {'x': x, 'ctx_1024': ctx_1024, 'L0_xattn_cos': _L0_xattn_in['cos'], 'L0_xattn_sin': _L0_xattn_in['sin'], 'L0_xattn_ln_lat_g': _L0_xattn_in['ln_lat_g'], 'L0_xattn_ln_lat_b': _L0_xattn_in['ln_lat_b'], 'L0_xattn_ln_ctx_g': _L0_xattn_in['ln_ctx_g'], 'L0_xattn_ln_ctx_b': _L0_xattn_in['ln_ctx_b'], 'L0_xattn_Wq': _L0_xattn_in['Wq'], 'L0_xattn_Wkv': _L0_xattn_in['Wkv'], 'L0_xattn_Wo': _L0_xattn_in['Wo'], 'L0_xattn_bo': _L0_xattn_in['bo'], 'L0_ffn_gamma1': _L0_ffn_in['gamma1'], 'L0_ffn_Wq': _L0_ffn_in['Wq'], 'L0_ffn_bq': _L0_ffn_in['bq'], 'L0_ffn_Wdown': _L0_ffn_in['Wdown'], 'L0_ffn_bdown': _L0_ffn_in['bdown'], 'L0_ffn_Wup': _L0_ffn_in['Wup'], 'L0_ffn_bup': _L0_ffn_in['bup'], 'L0_ffn_Wo': _L0_ffn_in['Wo'], 'L0_ffn_bo': _L0_ffn_in['bo'], 'L0_ffn_gamma2': _L0_ffn_in['gamma2'], 'L0_ffn_Wg': _L0_ffn_in['Wg'], 'L0_ffn_bg': _L0_ffn_in['bg'], 'L0_ffn_We': _L0_ffn_in['We']}

def reference(x, ctx_1024, L0_xattn_cos, L0_xattn_sin, L0_xattn_ln_lat_g, L0_xattn_ln_lat_b, L0_xattn_ln_ctx_g, L0_xattn_ln_ctx_b, L0_xattn_Wq, L0_xattn_Wkv, L0_xattn_Wo, L0_xattn_bo, L0_ffn_gamma1, L0_ffn_Wq, L0_ffn_bq, L0_ffn_Wdown, L0_ffn_bdown, L0_ffn_Wup, L0_ffn_bup, L0_ffn_Wo, L0_ffn_bo, L0_ffn_gamma2, L0_ffn_Wg, L0_ffn_bg, L0_ffn_We):
    import jax
    import jax.numpy as jnp

    def _L0_xattn_ref(latents, context, cos, sin, ln_lat_g, ln_lat_b, ln_ctx_g, ln_ctx_b, Wq, Wkv, Wo, bo):
        import jax, jax.numpy as jnp
        import numpy as np
        DIM = 128
        HEADS = 16
        DHEAD = 64
        INNER = HEADS * DHEAD
        EPS = 1e-05

        def layer_norm(x, g, b):
            mu = jnp.mean(x, axis=-1, keepdims=True)
            var = jnp.mean(jnp.square(x - mu), axis=-1, keepdims=True)
            return (x - mu) * jax.lax.rsqrt(var + EPS) * g + b

        def apply_rope(x, cos, sin):
            d2 = x.shape[-1] // 2
            x1, x2 = (x[..., :d2], x[..., d2:])
            return jnp.concatenate([x1 * cos - x2 * sin, x2 * cos + x1 * sin], axis=-1)
        b, n, _ = latents.shape
        s = context.shape[1]
        lat = layer_norm(latents, ln_lat_g, ln_lat_b)
        ctx = layer_norm(context, ln_ctx_g, ln_ctx_b)
        q = (lat @ Wq).reshape(b, n, HEADS, DHEAD).transpose(0, 2, 1, 3)
        kv = ctx @ Wkv
        k, v = jnp.split(kv, 2, axis=-1)
        k = k.reshape(b, s, HEADS, DHEAD).transpose(0, 2, 1, 3)
        v = v.reshape(b, s, HEADS, DHEAD).transpose(0, 2, 1, 3)
        k = apply_rope(k, cos[None, None], sin[None, None])
        scale = DHEAD ** (-0.5)
        attn = jnp.einsum('bhnd,bhsd->bhns', q, k) * scale
        attn = jnp.clip(attn, -11.0, 11.0)
        attn = jax.nn.softmax(attn, axis=-1)
        out = jnp.einsum('bhns,bhsd->bhnd', attn, v)
        out = out.transpose(0, 2, 1, 3).reshape(b, n, INNER)
        return out @ Wo + bo

    def _L0_ffn_ref(x, gamma1, Wq, bq, Wdown, bdown, Wup, bup, Wo, bo, gamma2, Wg, bg, We):
        import jax, jax.numpy as jnp
        import numpy as np
        D = 128
        H = 16
        HD = D // H
        L = 64
        E = 8
        B, T = (4, 256)
        EPS = 1e-06

        def _glorot(k, shape):
            fan_in, fan_out = (shape[-2], shape[-1])
            lim = np.sqrt(6.0 / (fan_in + fan_out)).astype(np.float32)
            return jax.random.uniform(k, shape, jnp.float32, -lim, lim)

        def _rmsnorm(x, gamma):
            return gamma * x * jax.lax.rsqrt(jnp.mean(x * x, axis=-1, keepdims=True) + EPS)
        b, t = (x.shape[0], x.shape[1])
        h = _rmsnorm(x, gamma1)
        q = (h @ Wq + bq).reshape(b, t, H, HD)
        kv = ((h @ Wdown + bdown) @ Wup + bup).reshape(b, t, H, 2 * HD)
        k, v = jnp.split(kv, 2, axis=-1)
        att = jnp.einsum('bthd,btgd->bthg', q, k) / np.sqrt(HD).astype(np.float32)
        att = jax.nn.softmax(att, axis=-1)
        out = jnp.einsum('bthg,btgd->bthd', att, v).reshape(b, t, D)
        x = x + (out @ Wo + bo)
        h2 = _rmsnorm(x, gamma2)
        gate = jax.nn.softmax(h2 @ Wg + bg, axis=-1)
        combined = jnp.einsum('btd,edf,bte->btf', h2, We, gate)
        return x + combined
    x = x + _L0_xattn_ref(_layernorm(x, axis=-1), ctx_1024, L0_xattn_cos, L0_xattn_sin, L0_xattn_ln_lat_g, L0_xattn_ln_lat_b, L0_xattn_ln_ctx_g, L0_xattn_ln_ctx_b, L0_xattn_Wq, L0_xattn_Wkv, L0_xattn_Wo, L0_xattn_bo)
    x = x + _L0_ffn_ref(_layernorm(x, axis=-1), L0_ffn_gamma1, L0_ffn_Wq, L0_ffn_bq, L0_ffn_Wdown, L0_ffn_bdown, L0_ffn_Wup, L0_ffn_bup, L0_ffn_Wo, L0_ffn_bo, L0_ffn_gamma2, L0_ffn_Wg, L0_ffn_bg, L0_ffn_We)
    return x

_drawn_inputs = setup_inputs


def setup_inputs(seed=0):
    import zlib

    import numpy as np

    out = dict(_drawn_inputs(seed))
    spreads = {'L0_xattn_ln_lat_g': (1.0, 0.6),
     'L0_xattn_ln_lat_b': (0.0, 0.623),
     'L0_xattn_ln_ctx_g': (1.0, 0.2),
     'L0_xattn_ln_ctx_b': (0.0, 0.1),
     'L0_xattn_bo': (0.0, 0.1),
     'L0_ffn_gamma1': (1.0, 0.2),
     'L0_ffn_bq': (0.0, 0.77),
     'L0_ffn_bdown': (0.0, 0.605),
     'L0_ffn_bup': (0.0, 0.326),
     'L0_ffn_bo': (0.0, 0.1),
     'L0_ffn_gamma2': (1.0, 0.2),
     'L0_ffn_bg': (0.0, 0.796)}
    factors = {'L0_xattn_cos': 4.04, 'L0_xattn_sin': 3.963}
    for name, (base, spread) in spreads.items():
        noise = np.random.default_rng([zlib.crc32(name.encode()), seed]).standard_normal(out[name].shape)
        drawn = base * np.exp(spread * noise) if base else spread * noise
        out[name] = jnp.asarray(drawn.astype(out[name].dtype))
    for name, factor in factors.items():
        out[name] = (out[name] * factor).astype(out[name].dtype)
    return out
```

```python
import concourse.bass as bass
from concourse import mybir
from contextlib import ExitStack

fp32 = mybir.dt.float32
fp32r = mybir.dt.float32r
ALU = mybir.AluOpType
ACT = mybir.ActivationFunctionType
AX = mybir.AxisListType.X

NB = 4
NT = 256
NS = 512
D = 128
H = 16
DH = 64
HALF = DH // 2
INNER = H * DH
PAIRS = H // 2
NPAIR = NB * PAIRS
TT = NT // 128
SC = NS // 128
LN_EPS = 1e-5
RMS_EPS = 1e-6
SCALE = DH ** -0.5
EXP_LOW = 1.6701700790245659e-05
EXP_HIGH = 59874.141715197818
G = 16
GD = D // G
L = 64
NE = 8
SCALE2 = GD ** -0.5
KV_AHEAD = 2
LAST_SLOT = NPAIR + 2 * PAIRS

POST_STEPS = {
    (1, "b"): "norm0", (1, "c"): "norm1", (2, "a"): "norm2", (2, "b"): "norm3", (2, "c"): "out_proj",
    (4, "a"): "h_T", (4, "b"): "query2", (4, "c"): "down", (5, "a"): "keyval2", (8, "c"): "o_T",
    (9, "a"): "out_proj2", (9, "d"): "h2_T", (10, "d"): "gate",
    (11, "d"): "moe0", (12, "d"): "moe1", (13, "d"): "moe2", (14, "d"): "moe3",
}
PREP_STEPS = {(5, "b"): "ctx_T", (6, "a"): "lat_T"}
FIRST_STEPS = [("ctx_T", 0), ("cos_T", 0), ("sin_T", 0), ("lat_T", 0)]


def side_step(slot, pos):
    for b in range(NB):
        name = POST_STEPS.get((slot - PAIRS * (b + 1), pos))
        if name:
            return name, b
        name = PREP_STEPS.get((slot - PAIRS * (b - 1), pos)) if b else None
        if name:
            return name, b
    return None


def side_order():
    order = list(FIRST_STEPS)
    for slot in range(-KV_AHEAD, LAST_SLOT):
        for pos in "abcd":
            if side_step(slot, pos):
                order.append(side_step(slot, pos))
    return {step: n for n, step in enumerate(order)}


SIDE = side_order()


def value_units(slot):
    b, p = divmod(slot, PAIRS)
    if p >= PAIRS - 2 and b + 1 < NB:
        first = 8 * (b + 1) + 2 * (p - (PAIRS - 2))
        return [first, first + 1]
    if 1 <= p <= 4 and 0 <= b < NB:
        return [8 * b + 3 + p]
    return []


def value_units_before(slot):
    return sum(len(value_units(s)) for s in range(-KV_AHEAD, slot))


def xattn_ffn(nc, x, ctx, cos, sin, ln_lat_g, ln_lat_b, ln_ctx_g, ln_ctx_b, Wq, Wkv, Wo, bo,
              gamma1, f_Wq, f_bq, f_Wdown, f_bdown, f_Wup, f_bup, f_Wo, f_bo, gamma2, f_Wg, f_bg, f_We, out):
    es = ExitStack()
    with es:
        def sb(name, shape, dt=fp32):
            return es.enter_context(nc.sbuf_tensor(name, shape, dt))

        def pb(name):
            return es.enter_context(nc.psum_tensor(name, [128, 512], fp32))

        def sem(name):
            return es.enter_context(nc.semaphore(name))

        x_in = sb("x_in", [128, NB * TT, D])
        ctx_in = sb("ctx_in", [128, 2, SC, D])
        cos_in = sb("cos_in", [128, SC, HALF])
        sin_in = sb("sin_in", [128, SC, HALF])
        prod = sb("prod", [128, TT, G * G * GD])
        wk_in, wv_in = (prod[:, 0, i * INNER:(i + 1) * INNER] for i in range(2))
        wq_in = prod[:, 1, 0:INNER]
        trig4 = prod[:, 1, INNER:2 * INNER].rearrange("p (w c r i) -> p w c r i", w=2, c=SC, r=4)
        cosT = sb("cosT", [128, NS])
        sinT = sb("sinT", [128, NS])
        vec = sb("vec", [128, 6])
        LAT_G, LAT_B, CTX_G, CTX_B, GAM1, GAM2 = (vec[:, i:i + 1] for i in range(6))
        bdown_c = sb("bdown_c", [L, 1])
        bo_r = sb("bo_r", [128, D])
        fbo_r = sb("fbo_r", [128, D])
        fbq_r = sb("fbq_r", [128, D])
        fbup_r = sb("fbup_r", [128, 2 * D])
        fbg_r = sb("fbg_r", [128, NE])
        ident = sb("ident", [128, 128])
        sum_rows = sb("sum_rows", [128, 120])
        spread = sb("spread", [128, PAIRS, 128], fp32r)
        wkA = sb("wkA", [128, 2, INNER], fp32r)
        wkB = sb("wkB", [128, 2, INNER], fp32r)
        wqD = sb("wqD", [128, 2, H, 2, DH], fp32r)
        wvS = sb("wvS", [128, 2, INNER], fp32r)
        wo = sb("wo", [128, PAIRS, D])
        fwq = sb("fwq", [128, D])
        fwdown = sb("fwdown", [128, L])
        fwup = sb("fwup", [L, 2 * D])
        fwo = sb("fwo", [128, D])
        fwg = sb("fwg", [128, NE])
        fwe = sb("fwe", [128, NE, D])
        c_stat = sb("c_stat", [128, SC, 6])
        c_mv = sb("c_mv", [128, SC, 2])
        c_rstd = sb("c_rstd", [128, SC])
        ctx_n = sb("ctx_n", [128, SC, D])
        l_stat = sb("l_stat", [128, TT, 6])
        l_mv = sb("l_mv", [128, TT, 2])
        l_rstd = sb("l_rstd", [128, TT])
        l2_mv = sb("l2_mv", [128, TT, 2])
        l2_rstd = sb("l2_rstd", [128, TT])
        lat_1 = sb("lat_1", [128, TT, D])
        lat_2 = sb("lat_2", [128, TT, D])
        ctxT_f = sb("ctxT_f", [128, NS])
        latT_f = sb("latT_f", [128, NT])
        ctxT = sb("ctxT", [128, 2, NS], fp32r)
        latT = sb("latT", [128, 2, NT], fp32r)
        kcos = sb("kcos", [128, 2, NS])
        ksin = sb("ksin", [128, 2, NS])
        krot = sb("krot", [128, 2, NS])
        ks = sb("ks", [128, 3, 2, NS], fp32r)
        qs = sb("qs", [128, 2, 2, 2, NT], fp32r)
        v = sb("v", [128, SC, INNER])
        e = sb("e", [128, 4, SC, NT])
        esum = sb("esum", [128, 4, 2, NT])
        u = sb("u", [128, PAIRS, NT])
        spread_f = u[:, :, 0:128]
        on = sb("on", [128, PAIRS, NT])
        moe = on[:, :, :].rearrange("p g n -> p (g n)").rearrange("p (t e d) -> p t e d", t=TT, e=NE)
        rec = sb("rec", [128, NT])
        recS = sb("recS", [128, 2, NT], fp32r)
        x2 = sb("x2", [128, TT, D])
        f_stat = sb("f_stat", [128, TT, 6])
        f_mv = sb("f_mv", [128, TT, 2])
        f_rstd = sb("f_rstd", [128, TT])
        xl = sb("xl", [128, TT, D])
        ss1 = sb("ss1", [128, TT])
        rr1 = sb("rr1", [128, TT])
        ss2 = sb("ss2", [128, TT])
        rr2 = sb("rr2", [128, TT])
        xlb = sb("xlb", [128, TT, D])
        hn = sb("hn", [128, TT, D])
        hT = sb("hT", [128, NT])
        q2 = sb("q2", [128, TT, D])
        dT = sb("dT", [L, NT])
        kv2 = sb("kv2", [128, TT, 2 * D])
        att = sb("att", [128, TT, G, G])
        amax = sb("amax", [128, TT, G])
        aden = sb("aden", [128, TT, G])
        o2 = sb("o2", [128, TT, D])
        x3 = sb("x3", [128, TT, D])
        h2T = sb("h2T", [128, NT])
        gl = sb("gl", [128, TT, NE])
        gmax = sb("gmax", [128, TT])
        gden = sb("gden", [128, TT])
        gate = sb("gate", [128, TT, NE])
        y = sb("y", [128, TT, D])
        half_p = sb("half_p", [128, SC])

        sc_bank = [pb(f"sc{i}") for i in range(3)]
        pj_a = pb("pj_a")
        pj_b = pb("pj_b")
        pv_bank = pb("pv")
        sum_bank = pb("sums")
        side = pb("side")

        ld = {n: sem(f"ld_{n}") for n in ("wk", "trig", "x", "vec", "wv", "wq", "bias", "wo", "ffn")}
        ld_ctx = [sem(f"ld_ctx{b}") for b in range(NB)]
        s_const = sem("s_const")
        s_trig = sem("s_trig")
        s_wkhi = sem("s_wkhi")
        s_wqhi = sem("s_wqhi")
        s_wvhi = sem("s_wvhi")
        s_wk = sem("s_wk")
        s_wq = sem("s_wq")
        s_wv = sem("s_wv")
        s_spread = sem("s_spread")
        s_cstat = sem("s_cstat")
        s_crstd = sem("s_crstd")
        s_ctxn = sem("s_ctxn")
        s_lstat = sem("s_lstat")
        s_lrstd = sem("s_lrstd")
        s_latn = sem("s_latn")
        s_ctxT = sem("s_ctxT")
        s_latT = sem("s_latT")
        s_side = sem("s_side")
        s_side_free = sem("s_side_free")
        s_kproj = sem("s_kproj")
        s_kmul = sem("s_kmul")
        s_krot = sem("s_krot")
        s_khi = sem("s_khi")
        s_klo = sem("s_klo")
        s_qproj = sem("s_qproj")
        s_qhi = sem("s_qhi")
        s_qlo = sem("s_qlo")
        s_vproj = sem("s_vproj")
        s_v = sem("s_v")
        s_score = sem("s_score")
        s_exp = sem("s_exp")
        s_clip = sem("s_clip")
        s_esum = sem("s_esum")
        s_pv = sem("s_pv")
        s_sum = sem("s_sum")
        s_u = sem("s_u")
        s_rec = sem("s_rec")
        s_recS = sem("s_recS")
        s_xb = sem("s_xb")
        s_fstat = sem("s_fstat")
        s_frstd = sem("s_frstd")
        s_xl = sem("s_xl")
        s_ss1 = sem("s_ss1")
        s_rr1 = sem("s_rr1")
        s_hn = sem("s_hn")
        s_xlb = sem("s_xlb")
        s_kv2 = sem("s_kv2")
        s_prod = sem("s_prod")
        s_attm = sem("s_attm")
        s_atte = sem("s_atte")
        s_pfree = sem("s_pfree")
        s_prod2 = sem("s_prod2")
        s_o2 = sem("s_o2")
        s_x3 = sem("s_x3")
        s_ss2 = sem("s_ss2")
        s_rr2 = sem("s_rr2")
        s_hn2 = sem("s_hn2")
        s_x23 = sem("s_x23")
        s_glm = sem("s_glm")
        s_gle = sem("s_gle")
        s_gate = sem("s_gate")
        s_moe = sem("s_moe")
        s_red = sem("s_red")
        s_y = sem("s_y")
        s_out = sem("s_out")
        own_dve = sem("own_dve")
        own_act = sem("own_act")
        own_pool = sem("own_pool")

        def f(ap):
            return ap.bitcast(fp32)

        block = es.enter_context(nc.Block())

        @block.sync
        def _(sp):
            x_v = x.rearrange("b (t p) d -> p (b t) d", p=128)
            ctx_v = ctx.rearrange("b (c p) d -> p (b c) d", p=128)
            out_v = out.rearrange("b (t p) d -> b p t d", p=128)
            def load_ctx(b):
                if b >= 2:
                    sp.wait_ge(s_ctxn, b - 1)
                sp.dma_start(ctx_in[:, b % 2, :, :], ctx_v[:, SC * b:SC * b + SC, :]).then_inc(ld_ctx[b], 16)

            load_ctx(0)
            sp.dma_start(wk_in, Wkv[:, 0:INNER]).then_inc(ld["wk"], 16)
            sp.dma_start(x_in[:, :, :], x_v).then_inc(ld["x"], 16)
            sp.dma_start(wq_in, Wq).then_inc(ld["wq"], 16)
            sp.dma_start(wv_in, Wkv[:, INNER:2 * INNER]).then_inc(ld["wv"], 16)
            load_ctx(1)
            sp.dma_start(wo[:, :, :], Wo.rearrange("(g p) n -> p g n", p=128)).then_inc(ld["wo"], 16)
            for dst, src in ((fwq[:, :], f_Wq), (fwdown[:, :], f_Wdown), (fwup[:, :], f_Wup), (fwo[:, :], f_Wo),
                             (fwg[:, :], f_Wg), (fwe[:, :, :], f_We.rearrange("e d f -> d e f"))):
                sp.dma_start(dst, src).then_inc(ld["ffn"], 16)
            for b in range(2, NB):
                load_ctx(b)
            for b in range(NB):
                sp.wait_ge(s_y, b + 1)
                sp.dma_start(out_v[b], y[:, :, :]).then_inc(s_out, 16)
                sp.wait_ge(s_out, 16 * (b + 1))

        @block.tensor
        def _(pe):
            def split3(out_ap, w_hi, w_lo, m_hi, m_lo):
                nc.tensor.matmul(out_ap, w_hi, m_hi, start=True, stop=False)
                nc.tensor.matmul(out_ap, w_hi, m_lo, start=False, stop=False)
                return nc.tensor.matmul(out_ap, w_lo, m_hi, start=False, stop=True)

            def keys(j):
                b, p = divmod(j, PAIRS)
                cols = slice(128 * p, 128 * p + 128)
                if p == 0:
                    pe.wait_ge(s_ctxT, b + 1)
                if j == 0:
                    pe.wait_ge(s_wk, 1)
                if j - KV_AHEAD >= 0:
                    pe.wait_ge(s_qlo, j - KV_AHEAD + 1)
                split3(pj_a[:, :], wkA[:, 0, cols], wkA[:, 1, cols], ctxT[:, 0, :], ctxT[:, 1, :]).then_inc(s_kproj, 1)
                done = value_units_before(j - KV_AHEAD)
                if done:
                    pe.wait_ge(s_v, done)
                split3(pj_b[:, :], wkB[:, 0, cols], wkB[:, 1, cols], ctxT[:, 0, :], ctxT[:, 1, :]).then_inc(s_kproj, 1)

            def queries(j):
                b, p = divmod(j, PAIRS)
                if p == 0:
                    pe.wait_ge(s_latT, b + 1)
                if j == 0:
                    pe.wait_ge(s_wq, 1)
                pe.wait_ge(s_kmul, 2 * min(j + 1, NPAIR - 1) + 1)
                for h in range(2):
                    w = wqD[:, :, 2 * p + h, :, :].rearrange("k s t d -> k s (t d)")
                    last = split3(pj_a[:, h * NT:(h + 1) * NT], w[:, 0, :], w[:, 1, :], latT[:, 0, :], latT[:, 1, :])
                last.then_inc(s_qproj, 1)

            def values(n, slot):
                b, unit = divmod(n, 8)
                half, c = divmod(unit, SC)
                if n == 0:
                    pe.wait_ge(s_wv, 1)
                if n:
                    pe.wait_ge(s_v, n)
                pe.wait_ge(s_kmul, 2 * min(slot + KV_AHEAD + 1, NPAIR))
                rows = slice(128 * c, 128 * c + 128)
                cols = slice(512 * half, 512 * half + 512)
                split3(pj_b[:, :], ctxT[:, 0, rows], ctxT[:, 1, rows], wvS[:, 0, cols], wvS[:, 1, cols])\
                    .then_inc(s_vproj, 1)

            def scores(j, h):
                if h == 0:
                    pe.wait_ge(s_klo, 2 * j + 2)
                    pe.wait_ge(s_qlo, j + 1)
                for half in range(2):
                    n = 4 * j + 2 * h + half
                    if n >= 3:
                        pe.wait_ge(s_exp, n - 2)
                    for c in range(2):
                        dst = sc_bank[n % 3][:, c * NT:(c + 1) * NT]
                        w = ks[:, j % 3, h, 128 * (2 * half + c):128 * (2 * half + c) + 128]
                        nc.tensor.matmul(dst, w, qs[:, j % 2, 0, h, :], start=True, stop=False)
                        last = nc.tensor.matmul(dst, w, qs[:, j % 2, 1, h, :], start=False, stop=True)
                    last.then_inc(s_score, 1)

            def times_values(j):
                b, p = divmod(j, PAIRS)
                pe.wait_ge(s_clip, 2 * j + 2)
                pe.wait_ge(s_v, 8 * b + (4 if p < PAIRS // 2 else 8))
                if j:
                    pe.wait_ge(s_u, j)
                for c in range(SC):
                    for h in range(2):
                        col = 128 * p + DH * h
                        last = nc.tensor.matmul(pv_bank[DH * h:DH * h + DH, 0:NT], v[:, c, col:col + DH],
                                                e[:, (2 * j + h) % 4, c, :], start=(c == 0), stop=(c == SC - 1))
                last.then_inc(s_pv, 1)
                pe.wait_ge(s_esum, 2 * j + 2)
                if p == 0 and b:
                    pe.wait_ge(s_rec, b)
                if j == 0:
                    pe.wait_ge(s_const, 2)
                w = sum_rows[:, 56 - 8 * p:120 - 8 * p]
                for c in range(2):
                    for h in range(2):
                        last = nc.tensor.matmul(sum_bank[DH * h:DH * h + DH, 0:NT], w, esum[:, (2 * j + h) % 4, c, :],
                                                start=(p == 0 and c == 0), stop=(p == PAIRS - 1 and c == 1))
                last.then_inc(s_sum, 1)

            def transposes(tiles):
                for t, tile in enumerate(tiles):
                    last = nc.tensor.transpose(side[:, 128 * t:128 * t + 128], tile, ident[:, :])
                return last

            def side_product(name, b):
                n = SIDE[name, b]
                if n:
                    pe.wait_ge(s_side_free, n)
                if name == "ctx_T":
                    if b == 0:
                        pe.wait_ge(s_const, 1)
                    pe.wait_ge(s_ctxn, b + 1)
                    last = transposes([ctx_n[:, c, :] for c in range(SC)])
                elif name in ("cos_T", "sin_T"):
                    which = int(name == "sin_T")
                    pe.wait_ge(s_trig, 4 * (which + 1))
                    last = transposes([trig4[:, which, c, :, :].rearrange("p r i -> p (r i)") for c in range(SC)])
                elif name == "lat_T":
                    pe.wait_ge(s_latn, b + 1)
                    last = transposes([lat_2[:, t, :] for t in range(TT)])
                elif name.startswith("norm"):
                    if name == "norm0":
                        pe.wait_ge(s_recS, b + 1)
                    if name == "norm0" and b == 0:
                        pe.wait_ge(s_spread, 1)
                    for i in range(2):
                        p = 2 * int(name[4]) + i
                        dst = side[:, i * NT:(i + 1) * NT]
                        nc.tensor.matmul(dst, spread[:, p, :], recS[:, 0, :], start=True, stop=False)
                        last = nc.tensor.matmul(dst, spread[:, p, :], recS[:, 1, :], start=False, stop=True)
                elif name == "out_proj":
                    if b == 0:
                        pe.wait_ge(ld["wo"], 16)
                    for t in range(TT):
                        for p in range(PAIRS):
                            last = nc.tensor.matmul(side[:, t * D:(t + 1) * D], on[:, p, 128 * t:128 * t + 128],
                                                    wo[:, p, :], start=(p == 0), stop=(p == PAIRS - 1))
                elif name == "h_T":
                    pe.wait_ge(s_hn, b + 1)
                    last = transposes([hn[:, t, :] for t in range(TT)])
                elif name == "query2":
                    if b == 0:
                        pe.wait_ge(ld["ffn"], 16 * 6)
                    for t in range(TT):
                        last = nc.tensor.matmul(side[:, t * D:(t + 1) * D], hT[:, 128 * t:128 * t + 128], fwq[:, :],
                                                start=True, stop=True)
                elif name == "down":
                    last = nc.tensor.matmul(side[0:L, 0:NT], fwdown[:, :], hT[:, :], start=True, stop=True)
                elif name == "keyval2":
                    for t in range(TT):
                        last = nc.tensor.matmul(side[:, 2 * D * t:2 * D * (t + 1)], dT[:, 128 * t:128 * t + 128],
                                                fwup[:, :], start=True, stop=True)
                elif name == "o_T":
                    pe.wait_ge(s_o2, b + 1)
                    last = transposes([o2[:, t, :] for t in range(TT)])
                elif name == "out_proj2":
                    for t in range(TT):
                        last = nc.tensor.matmul(side[:, t * D:(t + 1) * D], hT[:, 128 * t:128 * t + 128], fwo[:, :],
                                                start=True, stop=True)
                elif name == "h2_T":
                    pe.wait_ge(s_hn2, b + 1)
                    last = transposes([hn[:, t, :] for t in range(TT)])
                elif name == "gate":
                    for t in range(TT):
                        last = nc.tensor.matmul(side[:, t * NE:(t + 1) * NE], h2T[:, 128 * t:128 * t + 128], fwg[:, :],
                                                start=True, stop=True)
                elif name.startswith("moe"):
                    t, half = divmod(int(name[3]), 2)
                    w = fwe[:, 4 * half:4 * half + 4, :].rearrange("d e f -> d (e f)")
                    last = nc.tensor.matmul(side[:, :], h2T[:, 128 * t:128 * t + 128], w, start=True, stop=True)
                last.then_inc(s_side, 1)

            def side_at(slot, pos):
                step = side_step(slot, pos)
                if step:
                    side_product(*step)

            for name, b in FIRST_STEPS:
                side_product(name, b)
            for slot in range(-KV_AHEAD, LAST_SLOT):
                if slot + KV_AHEAD < NPAIR:
                    keys(slot + KV_AHEAD)
                if 0 <= slot < NPAIR:
                    scores(slot, 0)
                side_at(slot, "a")
                if 0 <= slot + 1 < NPAIR:
                    queries(slot + 1)
                if 0 <= slot < NPAIR:
                    scores(slot, 1)
                for n in value_units(slot):
                    values(n, slot)
                side_at(slot, "b")
                if 1 <= slot <= NPAIR:
                    times_values(slot - 1)
                side_at(slot, "c")
                side_at(slot, "d")

        @block.scalar
        def _(act):
            def own(ins):
                own.n += 1
                ins.then_inc(own_act, 1)
                act.wait_ge(own_act, own.n)
            own.n = 0

            act.dma_start(cos_in[:, :, :], cos.rearrange("(c p) i -> p c i", p=128)).then_inc(ld["trig"], 16)
            act.dma_start(sin_in[:, :, :], sin.rearrange("(c p) i -> p c i", p=128)).then_inc(ld["trig"], 16)
            for i, col in enumerate((ln_lat_g, ln_lat_b, ln_ctx_g, ln_ctx_b, gamma1, gamma2)):
                act.dma_start(vec[:, i:i + 1], col.rearrange("(p a) -> p a", a=1)).then_inc(ld["vec"], 16)
            act.dma_start(bdown_c[:, :], f_bdown.rearrange("(p a) -> p a", a=1)).then_inc(ld["vec"], 16)
            for dst, row in ((bo_r, bo), (fbo_r, f_bo), (fbq_r, f_bq), (fbup_r, f_bup), (fbg_r, f_bg)):
                act.dma_start(dst[:, :], row.rearrange("(a n) -> a n", a=1).to_broadcast([128, row.shape[0]]))\
                    .then_inc(ld["bias"], 16)

            def key_hi(j):
                act.wait_ge(s_krot, j + 1)
                if j >= 3:
                    act.wait_ge(s_score, 4 * (j - 3) + 4)
                for h in range(2):
                    rows = slice(DH * h, DH * h + DH)
                    nc.scalar.activation(ks[rows, j % 3, h, :], krot[rows, j % 2, :], ACT.Copy).then_inc(s_khi, 1)

            def query_hi(j):
                act.wait_ge(s_qproj, j + 1)
                if j >= 2:
                    act.wait_ge(s_score, 4 * (j - 2) + 4)
                nc.scalar.activation(qs[:, j % 2, 0, :, :].rearrange("p h n -> p (h n)"), pj_a[:, :], ACT.Copy)\
                    .then_inc(s_qhi, 1)

            def value_copy(n):
                b, unit = divmod(n, 8)
                half, c = divmod(unit, SC)
                act.wait_ge(s_vproj, n + 1)
                if b:
                    act.wait_ge(s_pv, PAIRS * (b - 1) + (PAIRS // 2 if half == 0 else PAIRS))
                nc.scalar.activation(v[:, c, 512 * half:512 * half + 512], pj_b[:, :], ACT.Copy).then_inc(s_v, 1)

            def exps(j, h):
                for half in range(2):
                    n = 4 * j + 2 * h + half
                    act.wait_ge(s_score, n + 1)
                    if j >= 2 and h == 0 and half == 0:
                        act.wait_ge(s_sum, j - 1)
                    nc.scalar.activation(e[:, (2 * j + h) % 4, 2 * half:2 * half + 2, :].rearrange("p c n -> p (c n)"),
                                         sc_bank[n % 3][:, :], ACT.Exp, scale=SCALE).then_inc(s_exp, 1)

            def attention_copy(j):
                act.wait_ge(s_pv, j + 1)
                if j >= PAIRS:
                    act.wait_ge(s_side_free, SIDE[f"norm{j % PAIRS // 2}", j // PAIRS - 1] + 1)
                nc.scalar.activation(u[:, j % PAIRS, :], pv_bank[:, 0:NT], ACT.Copy).then_inc(s_u, 1)

            def side_taken(slot, pos):
                step = side_step(slot, pos)
                if step:
                    take(*step)

            def take(name, b):
                full = SIDE[name, b] + 1
                if name == "ctx_T":
                    act.wait_ge(s_side, full)
                    if b == 0:
                        act.wait_ge(ld["vec"], 16 * 7)
                    else:
                        act.wait_ge(s_ctxT, b)
                    nc.scalar.activation(ctxT_f[:, :], side[:, :], ACT.Identity, scale=CTX_G, bias=CTX_B)\
                        .then_inc(s_side_free, 1)
                elif name in ("cos_T", "sin_T"):
                    act.wait_ge(s_side, full)
                    dst = cosT if name == "cos_T" else sinT
                    nc.scalar.activation(dst[:, :], side[:, :], ACT.Copy).then_inc(s_side_free, 1)
                elif name == "lat_T":
                    act.wait_ge(s_side, full)
                    if b:
                        act.wait_ge(s_latT, b)
                    nc.scalar.activation(latT_f[:, :], side[:, 0:NT], ACT.Identity, scale=LAT_G, bias=LAT_B)\
                        .then_inc(s_side_free, 1)
                elif name == "h_T":
                    act.wait_ge(s_side, full)
                    nc.scalar.activation(hT[:, :], side[:, 0:NT], ACT.Copy, scale=GAM1).then_inc(s_side_free, 1)
                elif name == "down":
                    act.wait_ge(s_side, full)
                    nc.scalar.activation(dT[:, :], side[0:L, 0:NT], ACT.Identity, bias=bdown_c[:, :])\
                        .then_inc(s_side_free, 1)
                elif name == "o_T":
                    act.wait_ge(s_side, full)
                    nc.scalar.activation(hT[:, :], side[:, 0:NT], ACT.Copy).then_inc(s_side_free, 1)
                elif name == "h2_T":
                    act.wait_ge(s_side, full)
                    nc.scalar.activation(h2T[:, :], side[:, 0:NT], ACT.Copy, scale=GAM2).then_inc(s_side_free, 1)
                elif name.startswith("moe"):
                    t, half = divmod(int(name[3]), 2)
                    if name == "moe0":
                        act.wait_ge(s_gate, b + 1)
                    if half == 0 and b:
                        act.wait_ge(s_red, 2 * (b - 1) + t + 1)
                    act.wait_ge(s_side, full)
                    for i in range(4):
                        last = nc.scalar.activation(moe[:, t, 4 * half + i, :], side[:, D * i:D * i + D], ACT.Copy,
                                                    scale=gate[:, t, 4 * half + i:4 * half + i + 1])
                        last.then_inc(s_side_free if i == 3 else s_moe, 1)

            act.wait_ge(ld["wk"], 16)
            nc.scalar.activation(wkA[:, 0, :], wk_in, ACT.Copy).then_inc(s_wkhi, 1)
            for name, b in FIRST_STEPS[:3]:
                take(name, b)
            act.wait_ge(ld["wq"], 16)
            wq_twice = wq_in.rearrange("k (h d) -> k h d", h=H)
            for t in range(2):
                nc.scalar.activation(wqD[:, 0, :, t, :], wq_twice, ACT.Copy).then_inc(s_wqhi, 1)
            take(*FIRST_STEPS[3])
            act.wait_ge(ld["wv"], 16)
            nc.scalar.activation(wvS[:, 0, :], wv_in, ACT.Copy).then_inc(s_wvhi, 1)

            for slot in range(-KV_AHEAD, LAST_SLOT):
                if 0 <= slot < NPAIR:
                    exps(slot, 0)
                side_taken(slot, "a")
                if 0 <= slot + 1 < NPAIR:
                    query_hi(slot + 1)
                if slot + KV_AHEAD < NPAIR:
                    key_hi(slot + KV_AHEAD)
                if 0 <= slot < NPAIR:
                    exps(slot, 1)
                for n in value_units(slot):
                    value_copy(n)
                side_taken(slot, "b")
                if 1 <= slot <= NPAIR:
                    attention_copy(slot - 1)
                side_taken(slot, "c")
                side_taken(slot, "d")
                for b in range(NB):
                    r = slot - PAIRS * (b + 1)
                    if r in (5, 6):
                        t = r - 5
                        act.wait_ge(s_attm, TT * b + t + 1)
                        a = att[:, t, :, :].rearrange("p h g -> p (h g)")
                        nc.scalar.activation(a, a, ACT.Exp, scale=SCALE2).then_inc(s_atte, 1)
                    if r == 10:
                        act.wait_ge(s_glm, b + 1)
                        a = gl[:, :, :].rearrange("p t n -> p (t n)")
                        nc.scalar.activation(a, a, ACT.Exp).then_inc(s_gle, 1)

        def products(engine, t):
            for hh in range(2):
                q_v = q2[:, t, :].rearrange("p (h d) -> p h d", h=G)[:, 8 * hh:8 * hh + 8, :]
                k_v = kv2[:, t, :].rearrange("p (g c) -> p g c", g=G)[:, :, 0:GD]
                last = engine.tensor_tensor(
                    prod[:, t, 1024 * hh:1024 * hh + 1024].rearrange("p (h g d) -> p h g d", h=G // 2, g=G),
                    q_v.unsqueeze(2).to_broadcast([128, G // 2, G, GD]),
                    k_v.unsqueeze(1).to_broadcast([128, G // 2, G, GD]), ALU.mult)
            return last

        def weighted_values(engine, t):
            for hh in range(2):
                v_v = kv2[:, t, :].rearrange("p (g c) -> p c g", g=G)[:, GD:2 * GD, :]
                last = engine.tensor_tensor(
                    prod[:, t, 1024 * hh:1024 * hh + 1024].rearrange("p (h d g) -> p h d g", h=G // 2, d=GD),
                    att[:, t, 8 * hh:8 * hh + 8, :].unsqueeze(2).to_broadcast([128, G // 2, GD, G]),
                    v_v.unsqueeze(1).to_broadcast([128, G // 2, GD, G]), ALU.mult)
            return last

        @block.vector
        def _(dve):
            def own(ins):
                own.n += 1
                ins.then_inc(own_dve, 1)
                dve.wait_ge(own_dve, own.n)
            own.n = 0

            def split_lo(dst, whole, hi):
                return nc.vector.tensor_tensor(dst, whole, f(hi), ALU.subtract)

            def statistics(mv, stat, tiles):
                for t, tile in enumerate(tiles):
                    last = nc.vector.bn_stats(stat[:, t, :], tile)
                own(last)
                for t in range(len(tiles)):
                    last = nc.vector.bn_aggr(mv[:, t, :], stat[:, t, :])
                return last

            def normalise(dst, src, mv, rstd, n):
                for t in range(n):
                    last = nc.vector.tensor_scalar(dst[:, t, :], src[:, t, :], mv[:, t, 0:1], rstd[:, t:t + 1],
                                                   ALU.subtract, ALU.mult)
                return last

            def ctx_statistics(b):
                dve.wait_ge(ld_ctx[b], 16)
                statistics(c_mv, c_stat, [ctx_in[:, b % 2, c, :] for c in range(SC)]).then_inc(s_cstat, 1)

            def ctx_normalise(b):
                dve.wait_ge(s_crstd, b + 1)
                if b:
                    dve.wait_ge(s_side, SIDE["ctx_T", b - 1] + 1)
                normalise(ctx_n, ctx_in[:, b % 2, :, :], c_mv, c_rstd, SC).then_inc(s_ctxn, 1)

            def tokens_statistics(b):
                if b == 0:
                    dve.wait_ge(ld["x"], 16)
                statistics(l_mv, l_stat, [x_in[:, TT * b + t, :] for t in range(TT)]).then_inc(s_lstat, 1)

            def tokens_first_norm(b):
                dve.wait_ge(s_lrstd, 2 * b + 1)
                own(normalise(lat_1, x_in[:, TT * b:TT * b + TT, :], l_mv, l_rstd, TT))
                statistics(l2_mv, l_stat, [lat_1[:, t, :] for t in range(TT)]).then_inc(s_lstat, 1)

            def tokens_second_norm(b):
                dve.wait_ge(s_lrstd, 2 * b + 2)
                if b:
                    dve.wait_ge(s_side, SIDE["lat_T", b - 1] + 1)
                normalise(lat_2, lat_1, l2_mv, l2_rstd, TT).then_inc(s_latn, 1)

            def split_ctxT(b):
                dve.wait_ge(s_side_free, SIDE["ctx_T", b] + 1)
                if b:
                    dve.wait_ge(s_kproj, 2 * PAIRS * b)
                    dve.wait_ge(s_vproj, 8 * b)
                own(nc.vector.tensor_copy(ctxT[:, 0, :], ctxT_f[:, :]))
                split_lo(ctxT[:, 1, :], ctxT_f[:, :], ctxT[:, 0, :]).then_inc(s_ctxT, 1)

            def split_latT(b):
                dve.wait_ge(s_side_free, SIDE["lat_T", b] + 1)
                if b:
                    dve.wait_ge(s_qproj, PAIRS * b)
                own(nc.vector.tensor_copy(latT[:, 0, :], latT_f[:, :]))
                split_lo(latT[:, 1, :], latT_f[:, :], latT[:, 0, :]).then_inc(s_latT, 1)

            def key_products(j):
                if j == 0:
                    dve.wait_ge(s_side_free, SIDE["sin_T", 0] + 1)
                if j >= 2:
                    dve.wait_ge(s_krot, j - 1)
                for i, (dst, bank, trig) in enumerate(((kcos, pj_a, cosT), (ksin, pj_b, sinT))):
                    dve.wait_ge(s_kproj, 2 * j + i + 1)
                    nc.vector.tensor_tensor(dst[:, j % 2, :], bank[:, :], trig[:, :], ALU.mult).then_inc(s_kmul, 1)

            def key_lo(j):
                for h in range(2):
                    dve.wait_ge(s_khi, 2 * j + h + 1)
                    own_rows = slice(DH * h, DH * h + DH)
                    other = slice(DH * (1 - h), DH * (1 - h) + DH)
                    split_lo(ks[other, j % 3, h, :], krot[own_rows, j % 2, :], ks[own_rows, j % 3, h, :])\
                        .then_inc(s_klo, 1)

            def query_lo(j):
                dve.wait_ge(s_qhi, j + 1)
                split_lo(qs[:, j % 2, 1, :, :].rearrange("p h n -> p (h n)"), pj_a[:, :],
                         qs[:, j % 2, 0, :, :].rearrange("p h n -> p (h n)")).then_inc(s_qlo, 1)

            def clip(j, h):
                dve.wait_ge(s_exp, 4 * j + 2 * h + 2)
                a = e[:, (2 * j + h) % 4, :, :].rearrange("p c n -> p (c n)")
                nc.vector.tensor_scalar(a, a, EXP_LOW, EXP_HIGH, ALU.max, ALU.min).then_inc(s_clip, 1)

            def reciprocals(b):
                dve.wait_ge(s_sum, PAIRS * (b + 1))
                nc.vector.reciprocal(rec[:, :], sum_bank[:, 0:NT]).then_inc(s_rec, 1)
                dve.wait_ge(s_rec, b + 1)
                own(nc.vector.tensor_copy(recS[:, 0, :], rec[:, :]))
                split_lo(recS[:, 1, :], rec[:, :], recS[:, 0, :]).then_inc(s_recS, 1)

            def side_taken(slot, pos):
                step = side_step(slot, pos)
                if step:
                    take(*step)

            def flat(ap):
                return ap.rearrange("p t n -> p (t n)")

            def twice(row):
                return row[:, :].unsqueeze(1).to_broadcast([128, TT, row.shape[1]])

            def square_sums(ss, src):
                for t in range(TT):
                    last = nc.vector.tensor_tensor_reduce(out=hn[:, t, :], in0=src[:, t, :], in1=src[:, t, :], scale=1.0,
                                                          scalar=0.0, op0=ALU.mult, op1=ALU.add,
                                                          accum_out=ss[:, t:t + 1])
                return last

            def take(name, b):
                full = SIDE[name, b] + 1
                if name.startswith("norm"):
                    i = int(name[4])
                    dve.wait_ge(s_u, PAIRS * b + 2 * i + 2)
                    if i == 0 and b:
                        dve.wait_ge(s_side, SIDE["out_proj", b - 1] + 1)
                    dve.wait_ge(s_side, full)
                    nc.vector.tensor_tensor(flat(on[:, 2 * i:2 * i + 2, :]), flat(u[:, 2 * i:2 * i + 2, :]),
                                            side[:, :], ALU.mult).then_inc(s_side_free, 1)
                elif name == "out_proj":
                    dve.wait_ge(s_xb, b + 1)
                    if b:
                        dve.wait_ge(s_x23, b)
                    dve.wait_ge(s_side, full)
                    nc.vector.tensor_tensor(flat(x2[:, :, :]), side[:, 0:NT],
                                            flat(x_in[:, TT * b:TT * b + TT, :]), ALU.add)\
                        .then_inc(s_side_free, 1)
                elif name == "query2":
                    if b == 0:
                        dve.wait_ge(ld["bias"], 16 * 5)
                    if b:
                        dve.wait_ge(s_prod, b)
                    dve.wait_ge(s_side, full)
                    nc.vector.tensor_tensor(q2[:, :, :], side[:, 0:NT].rearrange("p (t n) -> p t n", t=TT),
                                            twice(fbq_r), ALU.add).then_inc(s_side_free, 1)
                elif name == "keyval2":
                    if b:
                        dve.wait_ge(s_prod2, b)
                    dve.wait_ge(s_side, full)
                    nc.vector.tensor_tensor(kv2[:, :, :], side[:, :].rearrange("p (t n) -> p t n", t=TT),
                                            twice(fbup_r), ALU.add).then_inc(s_side_free, 1)
                    dve.wait_ge(s_side_free, full)
                elif name == "out_proj2":
                    dve.wait_ge(s_xlb, b + 1)
                    if b:
                        dve.wait_ge(s_x23, b)
                    dve.wait_ge(s_side, full)
                    nc.vector.tensor_tensor(flat(x3[:, :, :]), side[:, 0:NT], flat(xlb[:, :, :]), ALU.add)\
                        .then_inc(s_side_free, 1)
                    dve.wait_ge(s_side_free, full)
                    square_sums(ss2, x3).then_inc(s_ss2, 1)
                elif name == "gate":
                    dve.wait_ge(s_side, full)
                    nc.vector.tensor_tensor(gl[:, :, :], side[:, 0:TT * NE].rearrange("p (t n) -> p t n", t=TT),
                                            twice(fbg_r), ALU.add).then_inc(s_side_free, 1)
                    dve.wait_ge(s_side_free, full)
                    own(nc.vector.tensor_reduce(gmax[:, :], gl[:, :, :], AX, ALU.max))
                    nc.vector.tensor_tensor(gl[:, :, :], gl[:, :, :],
                                            gmax[:, :].unsqueeze(2).to_broadcast([128, TT, NE]),
                                            ALU.subtract).then_inc(s_glm, 1)
                    dve.wait_ge(s_gle, b + 1)
                    own(nc.vector.tensor_reduce(gden[:, :], gl[:, :, :], AX, ALU.add))
                    own(nc.vector.reciprocal(gden[:, :], gden[:, :]))
                    nc.vector.tensor_tensor(gate[:, :, :], gl[:, :, :],
                                            gden[:, :].unsqueeze(2).to_broadcast([128, TT, NE]),
                                            ALU.mult).then_inc(s_gate, 1)

            def reduce_logits(b, t):
                for hh in range(2):
                    pr = prod[:, t, 1024 * hh:1024 * hh + 1024].rearrange("p (h g d) -> p h g d", h=G // 2, g=G)
                    last = nc.vector.tensor_reduce(att[:, t, 8 * hh:8 * hh + 8, :], pr, AX, ALU.add)
                own(last)
                own(nc.vector.tensor_reduce(amax[:, t, :], att[:, t, :, :], AX, ALU.max))
                nc.vector.tensor_tensor(att[:, t, :, :], att[:, t, :, :],
                                        amax[:, t, :].unsqueeze(2).to_broadcast([128, G, G]),
                                        ALU.subtract).then_inc(s_attm, 1)

            def weight_sums(b, t):
                dve.wait_ge(s_atte, TT * b + t + 1)
                own(nc.vector.tensor_reduce(aden[:, t, :], att[:, t, :, :], AX, ALU.add))
                own(nc.vector.reciprocal(aden[:, t, :], aden[:, t, :]))

            def reduce_outputs(b, t):
                o_t = o2[:, t, :].rearrange("p (h d) -> p h d", h=G)
                for hh in range(2):
                    pr = prod[:, t, 1024 * hh:1024 * hh + 1024].rearrange("p (h d g) -> p h d g", h=G // 2, d=GD)
                    last = nc.vector.tensor_reduce(o_t[:, 8 * hh:8 * hh + 8, :], pr, AX, ALU.add)
                own(last)
                return nc.vector.tensor_tensor(o_t, o_t, aden[:, t, :].unsqueeze(2).to_broadcast([128, G, GD]),
                                               ALU.mult)

            def sum_experts(b, t):
                dve.wait_ge(s_side_free, SIDE[f"moe{2 * t + 1}", b] + 1)
                dve.wait_ge(s_moe, 6 * (TT * b + t + 1))
                if t == 0 and b:
                    dve.wait_ge(s_out, 16 * b)
                nc.vector.tensor_reduce(y[:, t, :], moe[:, t, :, :].rearrange("p n d -> p d n"), AX, ALU.add)\
                    .then_inc(s_red, 1)

            def second_layer(slot):
                for b in range(NB):
                    r = slot - PAIRS * (b + 1)
                    if r == 3:
                        dve.wait_ge(s_side_free, SIDE["out_proj", b] + 1)
                        statistics(f_mv, f_stat, [x2[:, t, :] for t in range(TT)]).then_inc(s_fstat, 1)
                        dve.wait_ge(s_frstd, b + 1)
                        if b:
                            dve.wait_ge(s_xlb, b)
                        normalise(xl, x2, f_mv, f_rstd, TT).then_inc(s_xl, 1)
                        dve.wait_ge(s_xl, b + 1)
                        if b:
                            dve.wait_ge(s_side, SIDE["h2_T", b - 1] + 1)
                        square_sums(ss1, xl).then_inc(s_ss1, 1)
                        dve.wait_ge(s_rr1, b + 1)
                        for t in range(TT):
                            last = nc.vector.tensor_scalar(hn[:, t, :], xl[:, t, :], rr1[:, t:t + 1], None, ALU.mult)
                        last.then_inc(s_hn, 1)
                    if r == 5:
                        own(products(nc.vector, 0))
                        reduce_logits(b, 0)
                    if r == 6:
                        dve.wait_ge(s_prod, b + 1)
                        reduce_logits(b, 1)
                        weight_sums(b, 0)
                        own(weighted_values(nc.vector, 0))
                    if r == 7:
                        reduce_outputs(b, 0)
                        weight_sums(b, 1)
                    if r == 8:
                        dve.wait_ge(s_prod2, b + 1)
                        reduce_outputs(b, 1).then_inc(s_o2, 1)
                    if r == 9:
                        dve.wait_ge(s_rr2, b + 1)
                        for t in range(TT):
                            last = nc.vector.tensor_scalar(hn[:, t, :], x3[:, t, :], rr2[:, t:t + 1], None, ALU.mult)
                        last.then_inc(s_hn2, 1)
                    if r == 13:
                        sum_experts(b, 0)
                    if r == 15:
                        sum_experts(b, 1)
                        dve.wait_ge(s_x23, b + 1)
                        dve.wait_ge(s_red, 2 * b + 2)
                        nc.vector.tensor_tensor(flat(y[:, :, :]), flat(y[:, :, :]), flat(x3[:, :, :]), ALU.add)\
                            .then_inc(s_y, 1)

            ctx_statistics(0)
            dve.wait_ge(ld["trig"], 32)
            for r in range(4):
                nc.vector.tensor_copy(trig4[:, 0, :, r, :], cos_in[:, :, :]).then_inc(s_trig, 1)
            for r in range(4):
                nc.vector.tensor_scalar(trig4[:, 1, :, r, :], sin_in[:, :, :], -1.0 if r % 2 == 0 else 1.0,
                                        None, ALU.mult).then_inc(s_trig, 1)
            ctx_normalise(0)
            tokens_statistics(0)
            dve.wait_ge(s_wkhi, 1)
            own(split_lo(wkA[:, 1, :], wk_in, wkA[:, 0, :]))
            split_ctxT(0)
            for s in range(2):
                src = f(wkA[:, s, :]).rearrange("k (h t i) -> k h t i", t=2, i=HALF)
                dst = wkB[:, s, :].rearrange("k (h t i) -> k h t i", t=2, i=HALF)
                for t in range(2):
                    last = nc.vector.tensor_copy(dst[:, :, t, :], src[:, :, 1 - t, :])
            last.then_inc(s_wk, 1)
            tokens_first_norm(0)
            tokens_second_norm(0)
            dve.wait_ge(s_wqhi, 2)
            wq_v = wq_in.rearrange("k (h d) -> k h d", h=H)
            for t in range(2):
                last = split_lo(wqD[:, 1, :, t, :], wq_v, wqD[:, 0, :, t, :])
            last.then_inc(s_wq, 1)
            split_latT(0)
            dve.wait_ge(s_wvhi, 1)
            split_lo(wvS[:, 1, :], wv_in, wvS[:, 0, :]).then_inc(s_wv, 1)

            for slot in range(-KV_AHEAD, LAST_SLOT):
                b, p = divmod(slot, PAIRS)
                if slot + KV_AHEAD < NPAIR:
                    key_products(slot + KV_AHEAD)
                if 0 <= slot < NPAIR:
                    clip(slot, 0)
                side_taken(slot, "a")
                if 0 <= slot + 1 < NPAIR:
                    query_lo(slot + 1)
                if slot + KV_AHEAD < NPAIR:
                    key_lo(slot + KV_AHEAD)
                if slot == 0:
                    dve.wait_ge(s_const, 3)
                    nc.vector.tensor_copy(spread[:, :, :], spread_f[:, :, :]).then_inc(s_spread, 1)
                if 0 <= slot < NPAIR:
                    clip(slot, 1)
                if 0 < b <= NB and p == 1:
                    reciprocals(b - 1)
                side_taken(slot, "b")
                second_layer(slot)
                if 0 <= b < NB - 1:
                    if p == 3:
                        ctx_statistics(b + 1)
                        tokens_statistics(b + 1)
                    if p == 4:
                        ctx_normalise(b + 1)
                        tokens_first_norm(b + 1)
                    if p == 5:
                        tokens_second_norm(b + 1)
                side_taken(slot, "c")
                side_taken(slot, "d")
                if 0 <= b < NB - 1:
                    if p == 5:
                        split_ctxT(b + 1)
                    if p == 6:
                        split_latT(b + 1)

        @block.gpsimd
        def _(pool):
            def own(ins):
                own.n += 1
                ins.then_inc(own_pool, 1)
                pool.wait_ge(own_pool, own.n)
            own.n = 0

            def inverse_root(dst, var, eps):
                own(nc.gpsimd.tensor_scalar_add(dst, var, eps))
                return nc.gpsimd.tensor_tensor(dst, dst, half_p[:, 0:dst.shape[1]], ALU.pow)

            def ctx_rstd(b):
                pool.wait_ge(s_cstat, b + 1)
                inverse_root(c_rstd[:, :], c_mv[:, :, 1], LN_EPS).then_inc(s_crstd, 1)

            def tokens_rstd(b, second):
                pool.wait_ge(s_lstat, 2 * b + 1 + second)
                dst, mv = ((l_rstd, l_mv), (l2_rstd, l2_mv))[second]
                inverse_root(dst[:, :], mv[:, :, 1], LN_EPS).then_inc(s_lrstd, 1)

            def mean_square_root(dst, ss):
                own(nc.gpsimd.tensor_scalar(dst[:, :], ss[:, :], 1.0 / D, RMS_EPS, ALU.mult, ALU.add))
                return nc.gpsimd.tensor_tensor(dst[:, :], dst[:, :], half_p[:, 0:TT], ALU.pow)

            own(nc.gpsimd.memset(half_p[:, :], -0.5))
            ctx_rstd(0)
            own(nc.gpsimd.memset(ident[:, :], 0.0))
            nc.gpsimd.affine_select(out=ident[:, :], in_=ident[:, :], compare_op=ALU.not_equal, fill=1.0, base=0,
                                    pattern=[[-1, 128]], channel_multiplier=1).then_inc(s_const, 1)
            tokens_rstd(0, 0)
            tokens_rstd(0, 1)
            own(nc.gpsimd.memset(sum_rows[:, :], 0.0))
            nc.gpsimd.memset(sum_rows[:, 56:64], 1.0).then_inc(s_const, 1)
            own(nc.gpsimd.memset(spread_f[:, :, :], 0.0))
            sp_v = spread_f[:, :, :].rearrange("k p (h c) -> k p h c", h=2)
            nc.gpsimd.affine_select(out=sp_v, in_=sp_v, compare_op=ALU.not_equal, fill=1.0, base=0,
                                    pattern=[[-8, PAIRS], [-DH, 2], [0, DH]], channel_multiplier=1)\
                .then_inc(s_const, 1)

            def rotate(j):
                pool.wait_ge(s_kmul, 2 * j + 2)
                if j >= 2:
                    pool.wait_ge(s_klo, 2 * (j - 1))
                nc.gpsimd.tensor_tensor(krot[:, j % 2, :], kcos[:, j % 2, :], ksin[:, j % 2, :], ALU.add)\
                    .then_inc(s_krot, 1)

            def chunk_sums(j, h):
                n = 2 * j + h
                pool.wait_ge(s_clip, n + 1)
                if j >= 2 and h == 0:
                    pool.wait_ge(s_sum, j - 1)
                nc.gpsimd.tensor_tensor(esum[:, n % 4, :, :], e[:, n % 4, 0:2, :], e[:, n % 4, 2:4, :], ALU.add)\
                    .then_inc(s_esum, 1)

            for slot in range(-KV_AHEAD, LAST_SLOT):
                b, p = divmod(slot, PAIRS)
                if slot + KV_AHEAD < NPAIR:
                    rotate(slot + KV_AHEAD)
                if 0 <= slot < NPAIR:
                    chunk_sums(slot, 0)
                for bb in range(NB):
                    r = slot - PAIRS * (bb + 1)
                    if r == 1:
                        if bb == 0:
                            pool.wait_ge(ld["bias"], 16 * 5)
                            pool.wait_ge(ld["x"], 16)
                        pool.wait_ge(s_latn, bb + 1)
                        nc.gpsimd.tensor_tensor(x_in[:, TT * bb:TT * bb + TT, :], x_in[:, TT * bb:TT * bb + TT, :],
                                                bo_r[:, :].unsqueeze(1).to_broadcast([128, TT, D]), ALU.add)\
                            .then_inc(s_xb, 1)
                    if r == 3:
                        pool.wait_ge(s_fstat, bb + 1)
                        inverse_root(f_rstd[:, :], f_mv[:, :, 1], LN_EPS).then_inc(s_frstd, 1)
                        pool.wait_ge(s_ss1, bb + 1)
                        mean_square_root(rr1, ss1).then_inc(s_rr1, 1)
                        if bb:
                            pool.wait_ge(s_side_free, SIDE["out_proj2", bb - 1] + 1)
                        nc.gpsimd.tensor_tensor(xlb[:, :, :], xl[:, :, :],
                                                fbo_r[:, :].unsqueeze(1).to_broadcast([128, TT, D]), ALU.add)\
                            .then_inc(s_xlb, 1)
                    if r == 5:
                        pool.wait_ge(s_side_free, SIDE["keyval2", bb] + 1)
                        products(nc.gpsimd, 1).then_inc(s_prod, 1)
                    if r == 7:
                        pool.wait_ge(s_atte, TT * bb + 2)
                        weighted_values(nc.gpsimd, 1).then_inc(s_prod2, 1)
                    if r == 9:
                        pool.wait_ge(s_ss2, bb + 1)
                        mean_square_root(rr2, ss2).then_inc(s_rr2, 1)
                        pool.wait_ge(s_hn2, bb + 1)
                        nc.gpsimd.tensor_tensor(x3[:, :, :], x2[:, :, :], x3[:, :, :], ALU.add).then_inc(s_x23, 1)
                if 0 <= slot < NPAIR:
                    chunk_sums(slot, 1)
                if 0 <= b < NB - 1:
                    if p == 3:
                        ctx_rstd(b + 1)
                        tokens_rstd(b + 1, 0)
                    if p == 4:
                        tokens_rstd(b + 1, 1)


_INS = ['x', 'ctx_1024', 'L0_xattn_cos', 'L0_xattn_sin', 'L0_xattn_ln_lat_g', 'L0_xattn_ln_lat_b',
        'L0_xattn_ln_ctx_g', 'L0_xattn_ln_ctx_b', 'L0_xattn_Wq', 'L0_xattn_Wkv', 'L0_xattn_Wo', 'L0_xattn_bo',
        'L0_ffn_gamma1', 'L0_ffn_Wq', 'L0_ffn_bq', 'L0_ffn_Wdown', 'L0_ffn_bdown', 'L0_ffn_Wup', 'L0_ffn_bup',
        'L0_ffn_Wo', 'L0_ffn_bo', 'L0_ffn_gamma2', 'L0_ffn_Wg', 'L0_ffn_bg', 'L0_ffn_We']
_OUTS = [((4, 256, 128), 'float32')]


def kernel(**inputs):
    import numpy as _np
    import concourse.bacc as _bacc
    from concourse import mybir as _mybir
    from concourse.bass_utils import run_bass_kernel_spmd as _run

    nc = _bacc.Bacc("TRN2", target_bir_lowering=False, num_devices=1)
    arrays, args = {}, []
    for name in _INS:
        a = _np.ascontiguousarray(inputs[name])
        arrays[f"in_{name}_dram"] = a
        args.append(nc.dram_tensor(f"in_{name}_dram", a.shape, _mybir.dt.from_np(a.dtype), kind="ExternalInput").ap())
    for i, (shape, dtype) in enumerate(_OUTS):
        dt = _mybir.dt.from_np(_np.dtype(dtype))
        args.append(nc.dram_tensor(f"out_{i}_dram", shape, dt, kind="ExternalOutput").ap())
    xattn_ffn(nc, *args)
    r = _run(nc, [arrays], core_ids=[0])
    got = tuple(r.results[0][f"out_{i}_dram"] for i in range(len(_OUTS)))
    return got[0]
```

```python
import concourse.bass as bass
from concourse import mybir
from contextlib import ExitStack

fp32 = mybir.dt.float32
fp32r = mybir.dt.float32r
ALU = mybir.AluOpType
ACT = mybir.ActivationFunctionType
AX = mybir.AxisListType.X

NB = 4
NT = 256
NS = 512
D = 128
H = 16
DH = 64
HALF = DH // 2
INNER = H * DH
PAIRS = H // 2
NPAIR = NB * PAIRS
TT = NT // 128
SC = NS // 128
LN_EPS = 1e-5
RMS_EPS = 1e-6
SCALE = DH ** -0.5
EXP_LOW = 1.6701700790245659e-05
EXP_HIGH = 59874.141715197818
G = 16
GD = D // G
L = 64
NE = 8
SCALE2 = GD ** -0.5
KV_AHEAD = 2
LAST_SLOT = NPAIR + 2 * PAIRS

POST_STEPS = {
    (0, "c"): "norm0", (1, "a"): "norm1", (1, "b"): "norm2", (1, "c"): "norm3", (2, "a"): "out_proj",
    (2, "c"): "h_T", (3, "a"): "query_down", (3, "c"): "keyval2", (8, "a"): "o_T", (8, "b"): "out_proj2",
    (10, "b"): "h2_T", (11, "b"): "gate", (12, "a"): "moe0", (12, "c"): "moe1", (13, "a"): "moe2", (13, "c"): "moe3",
}
PREP_STEPS = {(4, "b"): "ctx_T", (5, "b"): "lat_T"}
FIRST_STEPS = [("ctx_T", 0), ("cos_T", 0), ("sin_T", 0), ("lat_T", 0)]


def side_step(slot, pos):
    for b in range(NB):
        name = POST_STEPS.get((slot - PAIRS * (b + 1), pos))
        if name:
            return name, b
        name = PREP_STEPS.get((slot - PAIRS * (b - 1), pos)) if b else None
        if name:
            return name, b
    return None


TAIL_BANKS = {
    ("moe1", NB - 2): 1, ("moe3", NB - 2): 1,
    ("norm0", NB - 1): 1, ("norm1", NB - 1): 2, ("norm2", NB - 1): 3, ("norm3", NB - 1): 4, ("out_proj", NB - 1): 5,
    ("h_T", NB - 1): 2, ("query_down", NB - 1): 3, ("keyval2", NB - 1): 4, ("o_T", NB - 1): 2,
    ("out_proj2", NB - 1): 3, ("h2_T", NB - 1): 4, ("gate", NB - 1): 5,
    ("moe0", NB - 1): 0, ("moe1", NB - 1): 1, ("moe2", NB - 1): 2, ("moe3", NB - 1): 3,
}
SIDE_BANKS = 6


def side_order():
    steps = list(FIRST_STEPS)
    for slot in range(-KV_AHEAD, LAST_SLOT):
        for pos in "abc":
            if side_step(slot, pos):
                steps.append(side_step(slot, pos))
    order, used = {}, [0] * SIDE_BANKS
    for step in steps:
        k = TAIL_BANKS.get(step, 0)
        order[step] = (k, used[k])
        used[k] += 1
    return order


SIDE = side_order()


def value_units(slot):
    b, p = divmod(slot, PAIRS)
    if p >= PAIRS - 2 and b + 1 < NB:
        first = 8 * (b + 1) + 2 * (p - (PAIRS - 2))
        return [first, first + 1]
    if 1 <= p <= 4 and 0 <= b < NB:
        return [8 * b + 3 + p]
    return []


def value_units_before(slot):
    return sum(len(value_units(s)) for s in range(-KV_AHEAD, slot))


def xattn_ffn(nc, x, ctx, cos, sin, ln_lat_g, ln_lat_b, ln_ctx_g, ln_ctx_b, Wq, Wkv, Wo, bo,
              gamma1, f_Wq, f_bq, f_Wdown, f_bdown, f_Wup, f_bup, f_Wo, f_bo, gamma2, f_Wg, f_bg, f_We, out):
    es = ExitStack()
    with es:
        def sb(name, shape, dt=fp32):
            return es.enter_context(nc.sbuf_tensor(name, shape, dt))

        def pb(name):
            return es.enter_context(nc.psum_tensor(name, [128, 512], fp32))

        def sem(name):
            return es.enter_context(nc.semaphore(name))

        x_in = sb("x_in", [128, NB * TT, D])
        ctx_in = sb("ctx_in", [128, 2, SC, D])
        cos_in = sb("cos_in", [128, SC, HALF])
        sin_in = sb("sin_in", [128, SC, HALF])
        prod = sb("prod", [128, TT, G * G * GD])
        wk_in, wv_in = (prod[:, 0, i * INNER:(i + 1) * INNER] for i in range(2))
        wq_in = prod[:, 1, 0:INNER]
        trig4 = prod[:, 1, INNER:2 * INNER].rearrange("p (w c r i) -> p w c r i", w=2, c=SC, r=4)
        cosT = sb("cosT", [128, NS])
        sinT = sb("sinT", [128, NS])
        vec = sb("vec", [128, 6])
        CTX_G, CTX_B, LAT_G, LAT_B, GAM1, GAM2 = (vec[:, i:i + 1] for i in range(6))
        bdown_c = sb("bdown_c", [L, 1])
        bo_r = sb("bo_r", [128, D])
        fbo_r = sb("fbo_r", [128, D])
        fbq_r = sb("fbq_r", [128, D])
        fbup_r = sb("fbup_r", [128, 2 * D])
        fbg_r = sb("fbg_r", [128, NE])
        ident = sb("ident", [128, 128])
        sum_rows = sb("sum_rows", [128, 56])
        spread = sb("spread", [128, PAIRS, 128], fp32r)
        wkA = sb("wkA", [128, 2, INNER], fp32r)
        wkB = sb("wkB", [128, 2, INNER], fp32r)
        wqD = sb("wqD", [128, 2, H, 2, DH], fp32r)
        wvS = sb("wvS", [128, 2, INNER], fp32r)
        wo = sb("wo", [128, PAIRS, D])
        fwq = sb("fwq", [128, D])
        fwdown = sb("fwdown", [128, L])
        fwup = sb("fwup", [L, 2 * D])
        fwo = sb("fwo", [128, D])
        fwg = sb("fwg", [128, NE])
        fwe = sb("fwe", [128, NE, D])
        c_stat = sb("c_stat", [128, SC, 6])
        c_mv = sb("c_mv", [128, SC, 2])
        c_rstd = sb("c_rstd", [128, SC])
        ctx_n = sb("ctx_n", [128, SC, D])
        l_stat = sb("l_stat", [128, TT, 6])
        l_mv = sb("l_mv", [128, TT, 2])
        l_rstd = sb("l_rstd", [128, TT])
        l2_rstd = sb("l2_rstd", [128, TT])
        lat_2 = sb("lat_2", [128, TT, D])
        ctxT_f = sb("ctxT_f", [128, NS])
        latT_f = sb("latT_f", [128, NT])
        ctxT = sb("ctxT", [128, 2, NS], fp32r)
        latT = sb("latT", [128, 2, NT], fp32r)
        kcos = sb("kcos", [128, 2, NS])
        ksin = sb("ksin", [128, 2, NS])
        krot = sb("krot", [128, 2, NS])
        ks = sb("ks", [128, 3, 2, NS], fp32r)
        qs = sb("qs", [128, 2, 2, 2, NT], fp32r)
        v = sb("v", [128, SC, INNER])
        e = sb("e", [128, 4, SC, NT])
        esum = sb("esum", [128, 4, 2, NT])
        u = sb("u", [128, PAIRS, NT])
        spread_f = u[:, :, 0:128]
        on = sb("on", [128, PAIRS, NT])
        moe = on[:, :, :].rearrange("p g n -> p (g n)").rearrange("p (t e d) -> p t e d", t=TT, e=NE)
        rec = sb("rec", [128, NT])
        recS = sb("recS", [128, 2, NT], fp32r)
        f_stat = sb("f_stat", [128, TT, 6])
        f_mv = sb("f_mv", [128, TT, 2])
        f_rstd = sb("f_rstd", [128, TT])
        xl = sb("xl", [128, 2, TT, D])
        rr1 = sb("rr1", [128, TT])
        ss2 = sb("ss2", [128, TT])
        rr2 = sb("rr2", [128, TT])
        hn = sb("hn", [128, TT, D])
        hT = sb("hT", [128, NT])
        oT = sb("oT", [128, NT])
        hn2 = sb("hn2", [128, TT, D])
        q2 = sb("q2", [128, TT, D])
        dT = sb("dT", [L, NT])
        kv2 = sb("kv2", [128, TT, 2 * D])
        att = sb("att", [128, TT, G, G])
        amax = sb("amax", [128, TT, G])
        aden = sb("aden", [128, TT, G])
        o2 = sb("o2", [128, TT, D])
        h2T = sb("h2T", [128, NT])
        gl = sb("gl", [128, TT, NE])
        gmax = sb("gmax", [128, TT])
        gden = sb("gden", [128, TT])
        gate = sb("gate", [128, TT, NE])
        half_p = sb("half_p", [128, SC])

        sc_bank = [pb(f"sc{i}") for i in range(2)]
        pj_q = pb("pj_q")
        pj_k = [pb(f"pj_k{i}") for i in range(2)]
        pv_bank = pb("pv")
        sum_bank = pb("sums")
        side_banks = [pb("side")] + sc_bank + [pj_q] + pj_k

        ld = {n: sem(f"ld_{n}") for n in ("wk", "trig", "x", "wv", "wq", "bias", "wo", "ffn")}
        ld_ctx = [sem(f"ld_ctx{b}") for b in range(NB)]
        ld_vec = [sem(f"ld_vec{i}") for i in range(6)]
        s_const = sem("s_const")
        s_trig = sem("s_trig")
        s_wkhi = sem("s_wkhi")
        s_wqhi = sem("s_wqhi")
        s_wvhi = sem("s_wvhi")
        s_wk = sem("s_wk")
        s_wq = sem("s_wq")
        s_wv = sem("s_wv")
        s_spread = sem("s_spread")
        s_cstat = sem("s_cstat")
        s_crstd = sem("s_crstd")
        s_ctxn = sem("s_ctxn")
        s_lstat = sem("s_lstat")
        s_lrstd = sem("s_lrstd")
        s_latn = sem("s_latn")
        s_ctxT = sem("s_ctxT")
        s_latT = sem("s_latT")
        s_side = [sem(f"s_side{k}") for k in range(SIDE_BANKS)]
        s_side_free = [sem(f"s_side_free{k}") for k in range(SIDE_BANKS)]
        s_kproj = sem("s_kproj")
        s_kmul = sem("s_kmul")
        s_krot = sem("s_krot")
        s_khi = sem("s_khi")
        s_klo = sem("s_klo")
        s_qproj = sem("s_qproj")
        s_qhi = sem("s_qhi")
        s_qlo = sem("s_qlo")
        s_vproj = sem("s_vproj")
        s_v = sem("s_v")
        s_score = sem("s_score")
        s_exp = sem("s_exp")
        s_clip = sem("s_clip")
        s_esum = sem("s_esum")
        s_pv = sem("s_pv")
        s_sum = sem("s_sum")
        s_u = sem("s_u")
        s_rec = sem("s_rec")
        s_recS = sem("s_recS")
        s_xb = sem("s_xb")
        s_fstat = sem("s_fstat")
        s_frstd = sem("s_frstd")
        s_xl = sem("s_xl")
        s_hn = sem("s_hn")
        s_xlb = sem("s_xlb")
        s_q2 = sem("s_q2")
        s_prod = sem("s_prod")
        s_attm = sem("s_attm")
        s_atte = sem("s_atte")
        s_pfree = sem("s_pfree")
        s_prod2 = sem("s_prod2")
        s_o2 = sem("s_o2")
        s_x3 = sem("s_x3")
        s_ss2 = sem("s_ss2")
        s_rr2 = sem("s_rr2")
        s_hn2 = sem("s_hn2")
        s_x23 = sem("s_x23")
        s_mix = sem("s_mix")
        s_glm = sem("s_glm")
        s_gle = sem("s_gle")
        s_gate = sem("s_gate")
        s_moe = sem("s_moe")
        s_y = sem("s_y")
        s_out = sem("s_out")
        own_dve = sem("own_dve")
        own_act = sem("own_act")
        own_pool = sem("own_pool")

        def f(ap):
            return ap.bitcast(fp32)

        block = es.enter_context(nc.Block())

        def made(name, b):
            k, n = SIDE[name, b]
            return s_side[k], n + 1

        def taken(name, b):
            k, n = SIDE[name, b]
            return s_side_free[k], n + 1

        @block.sync
        def _(sp):
            x_v = x.rearrange("b (t p) d -> p (b t) d", p=128)
            ctx_v = ctx.rearrange("b (c p) d -> p (b c) d", p=128)
            out_v = out.rearrange("b (t p) d -> b p t d", p=128)
            def load_ctx(b):
                if b >= 2:
                    sp.wait_ge(s_ctxn, b - 1)
                sp.dma_start(ctx_in[:, b % 2, :, :], ctx_v[:, SC * b:SC * b + SC, :]).then_inc(ld_ctx[b], 16)

            load_ctx(0)
            sp.dma_start(wk_in, Wkv[:, 0:INNER]).then_inc(ld["wk"], 16)
            sp.dma_start(x_in[:, :, :], x_v).then_inc(ld["x"], 16)
            for i, col in enumerate((ln_ctx_g, ln_ctx_b, ln_lat_g, ln_lat_b, gamma1, gamma2)):
                sp.dma_start(vec[:, i:i + 1], col.rearrange("(p a) -> p a", a=1)).then_inc(ld_vec[i], 16)
            sp.dma_start(wq_in, Wq).then_inc(ld["wq"], 16)
            sp.dma_start(wv_in, Wkv[:, INNER:2 * INNER]).then_inc(ld["wv"], 16)
            load_ctx(1)
            sp.dma_start(wo[:, :, :], Wo.rearrange("(g p) n -> p g n", p=128)).then_inc(ld["wo"], 16)
            for dst, src in ((fwq[:, :], f_Wq), (fwdown[:, :], f_Wdown), (fwup[:, :], f_Wup), (fwo[:, :], f_Wo),
                             (fwg[:, :], f_Wg), (fwe[:, :, :], f_We.rearrange("e d f -> d e f"))):
                sp.dma_start(dst, src).then_inc(ld["ffn"], 16)
            sp.dma_start(bdown_c[:, :], f_bdown.rearrange("(p a) -> p a", a=1)).then_inc(ld["bias"], 16)
            for dst, row in ((bo_r, bo), (fbo_r, f_bo), (fbq_r, f_bq), (fbup_r, f_bup), (fbg_r, f_bg)):
                sp.dma_start(dst[:, :], row.rearrange("(a n) -> a n", a=1).to_broadcast([128, row.shape[0]]))\
                    .then_inc(ld["bias"], 16)
            for b in range(2, NB):
                load_ctx(b)
            for b in range(NB):
                if b < NB - 1:
                    sp.wait_ge(s_y, TT * (b + 1))
                else:
                    sp.wait_ge(s_mix, TT * NE)
                sp.dma_start(out_v[b], x_in[:, TT * b:TT * b + TT, :]).then_inc(s_out, 16)
            sp.wait_ge(s_out, 16 * NB)

        @block.tensor
        def _(pe):
            def split3(out_ap, w_hi, w_lo, m_hi, m_lo):
                nc.tensor.matmul(out_ap, w_hi, m_hi, start=True, stop=False)
                nc.tensor.matmul(out_ap, w_hi, m_lo, start=False, stop=False)
                return nc.tensor.matmul(out_ap, w_lo, m_hi, start=False, stop=True)

            def keys(j):
                b, p = divmod(j, PAIRS)
                cols = slice(128 * p, 128 * p + 128)
                if p == 0:
                    pe.wait_ge(s_ctxT, b + 1)
                if j == 0:
                    pe.wait_ge(s_wk, 1)
                done = value_units_before(j - KV_AHEAD)
                if done:
                    pe.wait_ge(s_v, done)
                if j:
                    pe.wait_ge(s_kmul, 2 * j)
                split3(pj_k[0][:, :], wkA[:, 0, cols], wkA[:, 1, cols], ctxT[:, 0, :], ctxT[:, 1, :]).then_inc(s_kproj, 1)
                split3(pj_k[1][:, :], wkB[:, 0, cols], wkB[:, 1, cols], ctxT[:, 0, :], ctxT[:, 1, :]).then_inc(s_kproj, 1)

            def queries(j):
                b, p = divmod(j, PAIRS)
                if p == 0:
                    pe.wait_ge(s_latT, b + 1)
                if j == 0:
                    pe.wait_ge(s_wq, 2)
                if j:
                    pe.wait_ge(s_qlo, j)
                for h in range(2):
                    w = wqD[:, :, 2 * p + h, :, :].rearrange("k s t d -> k s (t d)")
                    last = split3(pj_q[:, h * NT:(h + 1) * NT], w[:, 0, :], w[:, 1, :], latT[:, 0, :], latT[:, 1, :])
                last.then_inc(s_qproj, 1)

            def values(n, slot):
                b, unit = divmod(n, 8)
                half, c = divmod(unit, SC)
                if n == 0:
                    pe.wait_ge(s_wv, 1)
                if n >= 2:
                    pe.wait_ge(s_v, n - 1)
                pe.wait_ge(s_kmul, 2 * min(slot + KV_AHEAD + 1, NPAIR))
                rows = slice(128 * c, 128 * c + 128)
                cols = slice(512 * half, 512 * half + 512)
                split3(pj_k[n % 2][:, :], ctxT[:, 0, rows], ctxT[:, 1, rows], wvS[:, 0, cols], wvS[:, 1, cols])\
                    .then_inc(s_vproj, 1)

            def scores(j, h):
                if h == 0:
                    pe.wait_ge(s_klo, 2 * j + 2)
                    pe.wait_ge(s_qlo, j + 1)
                for half in range(2):
                    n = 4 * j + 2 * h + half
                    if n >= 2:
                        pe.wait_ge(s_exp, n - 1)
                    for c in range(2):
                        dst = sc_bank[n % 2][:, c * NT:(c + 1) * NT]
                        w = ks[:, j % 3, h, 128 * (2 * half + c):128 * (2 * half + c) + 128]
                        nc.tensor.matmul(dst, w, qs[:, j % 2, 0, h, :], start=True, stop=False)
                        last = nc.tensor.matmul(dst, w, qs[:, j % 2, 1, h, :], start=False, stop=True)
                    last.then_inc(s_score, 1)

            def times_values(j):
                b, p = divmod(j, PAIRS)
                pe.wait_ge(s_clip, 2 * j + 2)
                pe.wait_ge(s_v, 8 * b + (4 if p < PAIRS // 2 else 8))
                if j:
                    pe.wait_ge(s_u, j)
                for c in range(SC):
                    for h in range(2):
                        col = 128 * p + DH * h
                        last = nc.tensor.matmul(pv_bank[DH * h:DH * h + DH, 0:NT], v[:, c, col:col + DH],
                                                e[:, (2 * j + h) % 4, c, :], start=(c == 0), stop=(c == SC - 1))
                last.then_inc(s_pv, 1)

            def sums(j):
                b, p = divmod(j, PAIRS)
                if j < NPAIR - 1:
                    pe.wait_ge(s_esum, 2 * j + 2)
                    source, chunks = esum, 2
                else:
                    pe.wait_ge(s_clip, 2 * j + 2)
                    source, chunks = e, SC
                if p == 1 and b:
                    pe.wait_ge(s_rec, b)
                if j == 1:
                    pe.wait_ge(s_const, 2)
                w = sum_rows[:, 24 - 8 * (p // 2):56 - 8 * (p // 2)]
                for c in range(chunks):
                    for g in range(4):
                        last = nc.tensor.matmul(sum_bank[32 * g:32 * g + 32, 0:NT], w,
                                                source[:, (2 * (j - 1) + g) % 4, c, :],
                                                start=(p == 1 and c == 0), stop=(p == PAIRS - 1 and c == chunks - 1))
                last.then_inc(s_sum, 1)

            def transposes(side, tiles):
                for t, tile in enumerate(tiles):
                    last = nc.tensor.transpose(side[:, 128 * t:128 * t + 128], tile, ident[:, :])
                return last

            def side_product(name, b):
                k, n = SIDE[name, b]
                side = side_banks[k]
                source = {"out_proj": "norm3", "query_down": "h_T", "keyval2": "query_down", "out_proj2": "o_T",
                          "gate": "h2_T"}.get(name)
                if source:
                    pe.wait_ge(*taken(source, b))
                if n:
                    pe.wait_ge(s_side_free[k], n)
                elif 1 <= k <= 2:
                    pe.wait_ge(s_exp, 4 * NPAIR)
                elif k == 3:
                    pe.wait_ge(s_qlo, NPAIR)
                elif k >= 4:
                    pe.wait_ge(s_kmul, 2 * NPAIR)
                    pe.wait_ge(s_v, 8 * NB)
                if name == "ctx_T":
                    if b == 0:
                        pe.wait_ge(s_const, 1)
                    pe.wait_ge(s_ctxn, b + 1)
                    last = transposes(side, [ctx_n[:, c, :] for c in range(SC)])
                elif name in ("cos_T", "sin_T"):
                    which = int(name == "sin_T")
                    pe.wait_ge(s_trig, 4 * (which + 1))
                    last = transposes(side, [trig4[:, which, c, :, :].rearrange("p r i -> p (r i)") for c in range(SC)])
                elif name == "lat_T":
                    pe.wait_ge(s_latn, b + 1)
                    last = transposes(side, [lat_2[:, t, :] for t in range(TT)])
                elif name.startswith("norm"):
                    if name == "norm0":
                        pe.wait_ge(s_recS, b + 1)
                    if name == "norm0" and b == 0:
                        pe.wait_ge(s_spread, 1)
                    for i in range(2):
                        p = 2 * int(name[4]) + i
                        dst = side[:, i * NT:(i + 1) * NT]
                        nc.tensor.matmul(dst, spread[:, p, :], recS[:, 0, :], start=True, stop=False)
                        last = nc.tensor.matmul(dst, spread[:, p, :], recS[:, 1, :], start=False, stop=True)
                elif name == "out_proj":
                    if b == 0:
                        pe.wait_ge(ld["wo"], 16)
                    for t in range(TT):
                        for p in range(PAIRS):
                            last = nc.tensor.matmul(side[:, t * D:(t + 1) * D], on[:, p, 128 * t:128 * t + 128],
                                                    wo[:, p, :], start=(p == 0), stop=(p == PAIRS - 1))
                elif name == "h_T":
                    pe.wait_ge(s_hn, b + 1)
                    last = transposes(side, [hn[:, t, :] for t in range(TT)])
                elif name == "query_down":
                    if b == 0:
                        pe.wait_ge(ld["ffn"], 16 * 6)
                    for t in range(TT):
                        nc.tensor.matmul(side[:, t * D:(t + 1) * D], hT[:, 128 * t:128 * t + 128], fwq[:, :],
                                         start=True, stop=True)
                    last = nc.tensor.matmul(side[0:L, NT:2 * NT], fwdown[:, :], hT[:, :], start=True, stop=True)
                elif name == "keyval2":
                    for t in range(TT):
                        last = nc.tensor.matmul(side[:, 2 * D * t:2 * D * (t + 1)], dT[:, 128 * t:128 * t + 128],
                                                fwup[:, :], start=True, stop=True)
                elif name == "o_T":
                    pe.wait_ge(s_o2, b + 1)
                    last = transposes(side, [o2[:, t, :] for t in range(TT)])
                elif name == "out_proj2":
                    for t in range(TT):
                        last = nc.tensor.matmul(side[:, t * D:(t + 1) * D], oT[:, 128 * t:128 * t + 128], fwo[:, :],
                                                start=True, stop=True)
                elif name == "h2_T":
                    pe.wait_ge(s_hn2, b + 1)
                    last = transposes(side, [hn2[:, t, :] for t in range(TT)])
                elif name == "gate":
                    for t in range(TT):
                        last = nc.tensor.matmul(side[:, t * NE:(t + 1) * NE], h2T[:, 128 * t:128 * t + 128], fwg[:, :],
                                                start=True, stop=True)
                elif name.startswith("moe"):
                    t, half = divmod(int(name[3]), 2)
                    w = fwe[:, 4 * half:4 * half + 4, :].rearrange("d e f -> d (e f)")
                    last = nc.tensor.matmul(side[:, :], h2T[:, 128 * t:128 * t + 128], w, start=True, stop=True)
                last.then_inc(s_side[k], 1)

            def side_at(slot, pos):
                step = side_step(slot, pos)
                if step:
                    side_product(*step)

            for name, b in FIRST_STEPS:
                side_product(name, b)
            for slot in range(-KV_AHEAD, LAST_SLOT):
                if slot + KV_AHEAD < NPAIR:
                    keys(slot + KV_AHEAD)
                if 0 <= slot < NPAIR:
                    scores(slot, 0)
                if 2 <= slot <= NPAIR and slot % 2 == 0:
                    sums(slot - 1)
                side_at(slot, "a")
                if 0 <= slot + 1 < NPAIR:
                    queries(slot + 1)
                if 0 <= slot < NPAIR:
                    scores(slot, 1)
                for n in value_units(slot):
                    values(n, slot)
                side_at(slot, "b")
                if 1 <= slot <= NPAIR:
                    times_values(slot - 1)
                side_at(slot, "c")

        @block.scalar
        def _(act):
            def own(ins):
                own.n += 1
                ins.then_inc(own_act, 1)
                act.wait_ge(own_act, own.n)
            own.n = 0

            act.dma_start(cos_in[:, :, :], cos.rearrange("(c p) i -> p c i", p=128)).then_inc(ld["trig"], 16)
            act.dma_start(sin_in[:, :, :], sin.rearrange("(c p) i -> p c i", p=128)).then_inc(ld["trig"], 16)
            act.preload_act_table(ACT.Exp)

            def key_hi(j):
                act.wait_ge(s_krot, j + 1)
                if j >= 3:
                    act.wait_ge(s_score, 4 * (j - 3) + 4)
                for h in range(2):
                    rows = slice(DH * h, DH * h + DH)
                    nc.scalar.activation(ks[rows, j % 3, h, :], krot[rows, j % 2, :], ACT.Copy).then_inc(s_khi, 1)

            def query_hi(j):
                act.wait_ge(s_qproj, j + 1)
                if j >= 2:
                    act.wait_ge(s_score, 4 * (j - 2) + 4)
                nc.scalar.activation(qs[:, j % 2, 0, :, :].rearrange("p h n -> p (h n)"), pj_q[:, :], ACT.Copy)\
                    .then_inc(s_qhi, 1)

            def value_copy(n):
                b, unit = divmod(n, 8)
                half, c = divmod(unit, SC)
                act.wait_ge(s_vproj, n + 1)
                if b:
                    act.wait_ge(s_pv, PAIRS * (b - 1) + (PAIRS // 2 if half == 0 else PAIRS))
                nc.scalar.activation(v[:, c, 512 * half:512 * half + 512], pj_k[n % 2][:, :], ACT.Copy).then_inc(s_v, 1)

            def exps(j, h):
                for half in range(2):
                    n = 4 * j + 2 * h + half
                    act.wait_ge(s_score, n + 1)
                    if j >= 2 and h == 0 and half == 0:
                        act.wait_ge(s_pv, j - 1)
                        act.wait_ge(s_esum, 2 * (j - 1))
                    nc.scalar.activation(e[:, (2 * j + h) % 4, 2 * half:2 * half + 2, :].rearrange("p c n -> p (c n)"),
                                         sc_bank[n % 2][:, :], ACT.Exp, scale=SCALE).then_inc(s_exp, 1)

            def attention_copy(j):
                act.wait_ge(s_pv, j + 1)
                if j >= PAIRS:
                    act.wait_ge(*taken(f"norm{j % PAIRS // 2}", j // PAIRS - 1))
                nc.scalar.activation(u[:, j % PAIRS, :], pv_bank[:, 0:NT], ACT.Copy).then_inc(s_u, 1)

            def side_taken(slot, pos):
                step = side_step(slot, pos)
                if step:
                    take(*step)

            def take(name, b):
                k = SIDE[name, b][0]
                side, free = side_banks[k], s_side_free[k]
                if name == "ctx_T":
                    act.wait_ge(*made(name, b))
                    if b == 0:
                        act.wait_ge(ld_vec[0], 16)
                        act.wait_ge(ld_vec[1], 16)
                    else:
                        act.wait_ge(s_ctxT, b)
                    nc.scalar.activation(ctxT_f[:, :], side[:, :], ACT.Identity, scale=CTX_G, bias=CTX_B)\
                        .then_inc(free, 1)
                elif name in ("cos_T", "sin_T"):
                    act.wait_ge(*made(name, b))
                    dst = cosT if name == "cos_T" else sinT
                    nc.scalar.activation(dst[:, :], side[:, :], ACT.Copy).then_inc(free, 1)
                elif name == "lat_T":
                    act.wait_ge(*made(name, b))
                    if b == 0:
                        act.wait_ge(ld_vec[2], 16)
                        act.wait_ge(ld_vec[3], 16)
                    else:
                        act.wait_ge(s_latT, b)
                    nc.scalar.activation(latT_f[:, :], side[:, 0:NT], ACT.Identity, scale=LAT_G, bias=LAT_B)\
                        .then_inc(free, 1)
                elif name == "h_T":
                    if b == 0:
                        act.wait_ge(ld_vec[4], 16)
                    act.wait_ge(*made(name, b))
                    nc.scalar.activation(hT[:, :], side[:, 0:NT], ACT.Copy, scale=GAM1).then_inc(free, 1)
                elif name == "query_down":
                    if b == 0:
                        act.wait_ge(ld["bias"], 16 * 6)
                    act.wait_ge(s_q2, b + 1)
                    nc.scalar.activation(dT[:, :], side[0:L, NT:2 * NT], ACT.Identity, bias=bdown_c[:, :])\
                        .then_inc(free, 1)
                elif name == "o_T":
                    act.wait_ge(*made(name, b))
                    nc.scalar.activation(oT[:, :], side[:, 0:NT], ACT.Copy).then_inc(free, 1)
                elif name == "h2_T":
                    if b == 0:
                        act.wait_ge(ld_vec[5], 16)
                    act.wait_ge(*made(name, b))
                    nc.scalar.activation(h2T[:, :], side[:, 0:NT], ACT.Copy, scale=GAM2).then_inc(free, 1)
                elif name.startswith("moe") and b < NB - 1:
                    t, half = divmod(int(name[3]), 2)
                    if name == "moe0":
                        act.wait_ge(s_gate, b + 1)
                    if half == 0 and b:
                        act.wait_ge(s_y, TT * (b - 1) + t + 1)
                    act.wait_ge(*made(name, b))
                    for i in range(4):
                        last = nc.scalar.activation(moe[:, t, 4 * half + i, :], side[:, D * i:D * i + D], ACT.Copy,
                                                    scale=gate[:, t, 4 * half + i:4 * half + i + 1])
                        last.then_inc(free if i == 3 else s_moe, 1)

            act.wait_ge(ld["wk"], 16)
            nc.scalar.activation(wkA[:, 0, :], wk_in, ACT.Copy).then_inc(s_wkhi, 1)
            for name, b in FIRST_STEPS[:3]:
                take(name, b)
            act.wait_ge(ld["wq"], 16)
            wq_twice = wq_in.rearrange("k (h d) -> k h d", h=H)
            for t in range(2):
                nc.scalar.activation(wqD[:, 0, :, t, :], wq_twice, ACT.Copy).then_inc(s_wqhi, 1)
            take(*FIRST_STEPS[3])
            act.wait_ge(ld["wv"], 16)
            nc.scalar.activation(wvS[:, 0, :], wv_in, ACT.Copy).then_inc(s_wvhi, 1)

            def second_layer(slot):
                for b in range(NB):
                    r = slot - PAIRS * (b + 1)
                    if r in (5, 6):
                        t = r - 5
                        act.wait_ge(s_attm, TT * b + t + 1)
                        a = att[:, t, :, :].rearrange("p h g -> p (h g)")
                        nc.scalar.activation(a, a, ACT.Exp, scale=SCALE2).then_inc(s_atte, 1)

            def gate_exps(slot):
                for b in range(NB):
                    if slot - PAIRS * (b + 1) == 11:
                        act.wait_ge(s_glm, b + 1)
                        a = gl[:, :, :].rearrange("p t n -> p (t n)")
                        nc.scalar.activation(a, a, ACT.Exp).then_inc(s_gle, 1)

            for slot in range(-KV_AHEAD, LAST_SLOT):
                if 0 <= slot < NPAIR:
                    exps(slot, 0)
                side_taken(slot, "a")
                second_layer(slot)
                if 0 <= slot + 1 < NPAIR:
                    query_hi(slot + 1)
                if 0 <= slot < NPAIR:
                    exps(slot, 1)
                for n in value_units(slot):
                    value_copy(n)
                if slot + KV_AHEAD < NPAIR:
                    key_hi(slot + KV_AHEAD)
                side_taken(slot, "b")
                if 1 <= slot <= NPAIR:
                    attention_copy(slot - 1)
                side_taken(slot, "c")
                gate_exps(slot)

        def products(engine, t, hh):
            q_v = q2[:, t, :].rearrange("p (h d) -> p h d", h=G)[:, 8 * hh:8 * hh + 8, :]
            k_v = kv2[:, t, :].rearrange("p (g c) -> p g c", g=G)[:, :, 0:GD]
            return engine.tensor_tensor(
                prod[:, t, 1024 * hh:1024 * hh + 1024].rearrange("p (h g d) -> p h g d", h=G // 2, g=G),
                q_v.unsqueeze(2).to_broadcast([128, G // 2, G, GD]),
                k_v.unsqueeze(1).to_broadcast([128, G // 2, G, GD]), ALU.mult)

        def weighted_values(engine, t, hh):
            v_v = kv2[:, t, :].rearrange("p (g c) -> p c g", g=G)[:, GD:2 * GD, :]
            return engine.tensor_tensor(
                prod[:, t, 1024 * hh:1024 * hh + 1024].rearrange("p (h d g) -> p h d g", h=G // 2, d=GD),
                att[:, t, 8 * hh:8 * hh + 8, :].unsqueeze(2).to_broadcast([128, G // 2, GD, G]),
                v_v.unsqueeze(1).to_broadcast([128, G // 2, GD, G]), ALU.mult)

        @block.vector
        def _(dve):
            def own(ins):
                own.n += 1
                ins.then_inc(own_dve, 1)
                dve.wait_ge(own_dve, own.n)
            own.n = 0

            def split_lo(dst, whole, hi):
                return nc.vector.tensor_tensor(dst, whole, f(hi), ALU.subtract)

            def statistics(mv, stat, tiles):
                for t, tile in enumerate(tiles):
                    last = nc.vector.bn_stats(stat[:, t, :], tile)
                own(last)
                for t in range(len(tiles)):
                    last = nc.vector.bn_aggr(mv[:, t, :], stat[:, t, :])
                return last

            def normalise(dst, src, mv, rstd, n):
                for t in range(n):
                    last = nc.vector.tensor_scalar(dst[:, t, :], src[:, t, :], mv[:, t, 0:1], rstd[:, t:t + 1],
                                                   ALU.subtract, ALU.mult)
                return last

            def ctx_statistics(b):
                dve.wait_ge(ld_ctx[b], 16)
                statistics(c_mv, c_stat, [ctx_in[:, b % 2, c, :] for c in range(SC)]).then_inc(s_cstat, 1)

            def ctx_normalise(b):
                dve.wait_ge(s_crstd, b + 1)
                if b:
                    dve.wait_ge(*made("ctx_T", b - 1))
                normalise(ctx_n, ctx_in[:, b % 2, :, :], c_mv, c_rstd, SC).then_inc(s_ctxn, 1)

            def tokens_statistics(b):
                if b == 0:
                    dve.wait_ge(ld["x"], 16)
                statistics(l_mv, l_stat, [x_in[:, TT * b + t, :] for t in range(TT)]).then_inc(s_lstat, 1)

            def tokens_normalise(b):
                dve.wait_ge(s_lrstd, b + 1)
                if b:
                    dve.wait_ge(*made("lat_T", b - 1))
                normalise(lat_2, x_in[:, TT * b:TT * b + TT, :], l_mv, l2_rstd, TT).then_inc(s_latn, 1)

            def split_ctxT(b):
                dve.wait_ge(*taken("ctx_T", b))
                if b:
                    dve.wait_ge(s_kproj, 2 * PAIRS * b)
                    dve.wait_ge(s_vproj, 8 * b)
                own(nc.vector.tensor_copy(ctxT[:, 0, :], ctxT_f[:, :]))
                split_lo(ctxT[:, 1, :], ctxT_f[:, :], ctxT[:, 0, :]).then_inc(s_ctxT, 1)

            def split_latT(b):
                dve.wait_ge(*taken("lat_T", b))
                if b:
                    dve.wait_ge(s_qproj, PAIRS * b)
                own(nc.vector.tensor_copy(latT[:, 0, :], latT_f[:, :]))
                split_lo(latT[:, 1, :], latT_f[:, :], latT[:, 0, :]).then_inc(s_latT, 1)

            def key_products(j):
                if j == 0:
                    dve.wait_ge(*taken("sin_T", 0))
                if j >= 2:
                    dve.wait_ge(s_krot, j - 1)
                for i, (dst, bank, trig) in enumerate(((kcos, pj_k[0], cosT), (ksin, pj_k[1], sinT))):
                    dve.wait_ge(s_kproj, 2 * j + i + 1)
                    nc.vector.tensor_tensor(dst[:, j % 2, :], bank[:, :], trig[:, :], ALU.mult).then_inc(s_kmul, 1)

            def key_lo(j):
                for h in range(2):
                    dve.wait_ge(s_khi, 2 * j + h + 1)
                    own_rows = slice(DH * h, DH * h + DH)
                    other = slice(DH * (1 - h), DH * (1 - h) + DH)
                    split_lo(ks[other, j % 3, h, :], krot[own_rows, j % 2, :], ks[own_rows, j % 3, h, :])\
                        .then_inc(s_klo, 1)

            def query_lo(j):
                dve.wait_ge(s_qhi, j + 1)
                split_lo(qs[:, j % 2, 1, :, :].rearrange("p h n -> p (h n)"), pj_q[:, :],
                         qs[:, j % 2, 0, :, :].rearrange("p h n -> p (h n)")).then_inc(s_qlo, 1)

            def clip(j, h):
                dve.wait_ge(s_exp, 4 * j + 2 * h + 2)
                a = e[:, (2 * j + h) % 4, :, :].rearrange("p c n -> p (c n)")
                nc.vector.tensor_scalar(a, a, EXP_LOW, EXP_HIGH, ALU.max, ALU.min).then_inc(s_clip, 1)

            def reciprocals(b):
                dve.wait_ge(s_sum, PAIRS // 2 * (b + 1))
                nc.vector.reciprocal(rec[:, :], sum_bank[:, 0:NT]).then_inc(s_rec, 1)
                dve.wait_ge(s_rec, b + 1)
                own(nc.vector.tensor_copy(recS[:, 0, :], rec[:, :]))
                split_lo(recS[:, 1, :], rec[:, :], recS[:, 0, :]).then_inc(s_recS, 1)

            def tokens(b):
                return x_in[:, TT * b:TT * b + TT, :]

            def side_taken(slot, pos):
                step = side_step(slot, pos)
                if step:
                    take(*step)

            def flat(ap):
                return ap.rearrange("p t n -> p (t n)")

            def twice(row):
                return row[:, :].unsqueeze(1).to_broadcast([128, TT, row.shape[1]])

            def square_sums(ss, src):
                for t in range(TT):
                    last = nc.vector.tensor_tensor_reduce(out=hn2[:, t, :], in0=src[:, t, :], in1=src[:, t, :], scale=1.0,
                                                          scalar=0.0, op0=ALU.mult, op1=ALU.add,
                                                          accum_out=ss[:, t:t + 1])
                return last

            def take(name, b):
                k = SIDE[name, b][0]
                side, free = side_banks[k], s_side_free[k]
                if name.startswith("norm"):
                    i = int(name[4])
                    dve.wait_ge(s_u, PAIRS * b + 2 * i + 2)
                    if i == 0 and b:
                        dve.wait_ge(*made("out_proj", b - 1))
                    if i == 0 and b >= 2:
                        dve.wait_ge(s_y, TT * (b - 1))
                    dve.wait_ge(*made(name, b))
                    nc.vector.tensor_tensor(flat(on[:, 2 * i:2 * i + 2, :]), flat(u[:, 2 * i:2 * i + 2, :]),
                                            side[:, :], ALU.mult).then_inc(free, 1)
                elif name == "out_proj":
                    dve.wait_ge(s_xb, b + 1)
                    dve.wait_ge(*made(name, b))
                    nc.vector.tensor_tensor(flat(tokens(b)), side[:, 0:NT], flat(tokens(b)), ALU.add)\
                        .then_inc(free, 1)
                elif name == "query_down":
                    if b == 0:
                        dve.wait_ge(ld["bias"], 16 * 6)
                    if b:
                        dve.wait_ge(s_prod, b)
                    dve.wait_ge(*made(name, b))
                    nc.vector.tensor_tensor(q2[:, :, :], side[:, 0:NT].rearrange("p (t n) -> p t n", t=TT),
                                            twice(fbq_r), ALU.add).then_inc(s_q2, 1)
                elif name == "keyval2":
                    if b:
                        dve.wait_ge(s_prod2, b)
                    dve.wait_ge(*made(name, b))
                    nc.vector.tensor_tensor(kv2[:, :, :], side[:, :].rearrange("p (t n) -> p t n", t=TT),
                                            twice(fbup_r), ALU.add).then_inc(free, 1)
                    dve.wait_ge(*taken(name, b))
                elif name == "out_proj2":
                    dve.wait_ge(s_xlb, b + 1)
                    dve.wait_ge(*made(name, b))
                    nc.vector.tensor_tensor(flat(xl[:, b % 2, :, :]), side[:, 0:NT], flat(xl[:, b % 2, :, :]), ALU.add)\
                        .then_inc(free, 1)
                    dve.wait_ge(*taken(name, b))
                    square_sums(ss2, xl[:, b % 2, :, :]).then_inc(s_ss2, 1)
                elif name == "gate":
                    dve.wait_ge(*made(name, b))
                    nc.vector.tensor_tensor(gl[:, :, :], side[:, 0:TT * NE].rearrange("p (t n) -> p t n", t=TT),
                                            twice(fbg_r), ALU.add).then_inc(free, 1)
                    dve.wait_ge(*taken(name, b))
                    own(nc.vector.tensor_reduce(gmax[:, :], gl[:, :, :], AX, ALU.max))
                    nc.vector.tensor_tensor(gl[:, :, :], gl[:, :, :],
                                            gmax[:, :].unsqueeze(2).to_broadcast([128, TT, NE]),
                                            ALU.subtract).then_inc(s_glm, 1)

            def gates(b):
                dve.wait_ge(s_gle, b + 1)
                own(nc.vector.tensor_reduce(gden[:, :], gl[:, :, :], AX, ALU.add))
                own(nc.vector.reciprocal(gden[:, :], gden[:, :]))
                nc.vector.tensor_tensor(gate[:, :, :], gl[:, :, :], gden[:, :].unsqueeze(2).to_broadcast([128, TT, NE]),
                                        ALU.mult).then_inc(s_gate, 1)

            def reduce_logits(b, t):
                for hh in range(2):
                    pr = prod[:, t, 1024 * hh:1024 * hh + 1024].rearrange("p (h g d) -> p h g d", h=G // 2, g=G)
                    last = nc.vector.tensor_reduce(att[:, t, 8 * hh:8 * hh + 8, :], pr, AX, ALU.add)
                own(last)
                own(nc.vector.tensor_reduce(amax[:, t, :], att[:, t, :, :], AX, ALU.max))
                nc.vector.tensor_tensor(att[:, t, :, :], att[:, t, :, :],
                                        amax[:, t, :].unsqueeze(2).to_broadcast([128, G, G]),
                                        ALU.subtract).then_inc(s_attm, 1)

            def weight_sums(b, t):
                dve.wait_ge(s_atte, TT * b + t + 1)
                own(nc.vector.tensor_reduce(aden[:, t, :], att[:, t, :, :], AX, ALU.add))
                own(nc.vector.reciprocal(aden[:, t, :], aden[:, t, :]))

            def reduce_outputs(b, t):
                o_t = o2[:, t, :].rearrange("p (h d) -> p h d", h=G)
                for hh in range(2):
                    pr = prod[:, t, 1024 * hh:1024 * hh + 1024].rearrange("p (h d g) -> p h d g", h=G // 2, d=GD)
                    last = nc.vector.tensor_reduce(o_t[:, 8 * hh:8 * hh + 8, :], pr, AX, ALU.add)
                own(last)
                return nc.vector.tensor_tensor(o_t, o_t, aden[:, t, :].unsqueeze(2).to_broadcast([128, G, GD]),
                                               ALU.mult)

            def layer_norm_statistics(b):
                dve.wait_ge(*taken("out_proj", b))
                statistics(f_mv, f_stat, [tokens(b)[:, t, :] for t in range(TT)]).then_inc(s_fstat, 1)

            def layer_norm(b):
                dve.wait_ge(s_frstd, b + 1)
                normalise(hn, tokens(b), f_mv, rr1, TT).then_inc(s_hn, 1)
                if b >= 2:
                    dve.wait_ge(s_x23, b - 1)
                normalise(xl[:, b % 2, :, :], tokens(b), f_mv, f_rstd, TT).then_inc(s_xl, 1)

            def root_norm(b):
                dve.wait_ge(s_rr2, b + 1)
                for t in range(TT):
                    last = nc.vector.tensor_scalar(hn2[:, t, :], xl[:, b % 2, t, :], rr2[:, t:t + 1], None, ALU.mult)
                last.then_inc(s_hn2, 1)

            def mix_experts(b):
                dve.wait_ge(s_x23, b + 1)
                dve.wait_ge(s_gate, b + 1)
                for i in range(NE):
                    for t in range(TT):
                        if i % 4 == 0:
                            dve.wait_ge(*made(f"moe{2 * t + i // 4}", b))
                        if i:
                            dve.wait_ge(s_mix, TT * (i - 1) + t + 1)
                        side = side_banks[SIDE[f"moe{2 * t + i // 4}", b][0]]
                        row = x_in[:, TT * b + t, :]
                        nc.vector.scalar_tensor_tensor(row, side[:, D * (i % 4):D * (i % 4) + D],
                                                       gate[:, t, i:i + 1], row, ALU.mult, ALU.add).then_inc(s_mix, 1)

            def second_layer(slot, when):
                for b in range(NB):
                    r = slot - PAIRS * (b + 1)
                    if (r, when) == (0, "late"):
                        reciprocals(b)
                    if (r, when) == (2, "early"):
                        layer_norm_statistics(b)
                    if (r, when) == (2, "late"):
                        layer_norm(b)
                    if (r, when) == (3, "end"):
                        for hh in range(2):
                            last = products(nc.vector, 0, hh)
                        own(last)
                    if (r, when) == (4, "late"):
                        reduce_logits(b, 0)
                    if (r, when) == (5, "late"):
                        dve.wait_ge(s_prod, b + 1)
                        reduce_logits(b, 1)
                        weight_sums(b, 0)
                        for hh in range(2):
                            last = weighted_values(nc.vector, 0, hh)
                        own(last)
                    if (r, when) == (6, "late"):
                        weight_sums(b, 1)
                        reduce_outputs(b, 0)
                    if (r, when) == (7, "late"):
                        dve.wait_ge(s_prod2, b + 1)
                        reduce_outputs(b, 1).then_inc(s_o2, 1)
                    if (r, when) == (10, "first"):
                        root_norm(b)
                    if (r, when) == (12, "first"):
                        gates(b)
                    if (r, when) == (13, "late") and b == NB - 1:
                        mix_experts(b)

            ctx_statistics(0)
            dve.wait_ge(ld["trig"], 32)
            for r in range(4):
                nc.vector.tensor_copy(trig4[:, 0, :, r, :], cos_in[:, :, :]).then_inc(s_trig, 1)
            for r in range(4):
                nc.vector.tensor_scalar(trig4[:, 1, :, r, :], sin_in[:, :, :], -1.0 if r % 2 == 0 else 1.0,
                                        None, ALU.mult).then_inc(s_trig, 1)
            ctx_normalise(0)
            tokens_statistics(0)
            dve.wait_ge(s_wkhi, 1)
            own(split_lo(wkA[:, 1, :], wk_in, wkA[:, 0, :]))
            split_ctxT(0)
            for s in range(2):
                src = f(wkA[:, s, :]).rearrange("k (h t i) -> k h t i", t=2, i=HALF)
                dst = wkB[:, s, :].rearrange("k (h t i) -> k h t i", t=2, i=HALF)
                for t in range(2):
                    last = nc.vector.tensor_copy(dst[:, :, t, :], src[:, :, 1 - t, :])
            last.then_inc(s_wk, 1)
            tokens_normalise(0)
            dve.wait_ge(s_wqhi, 2)
            wq_v = wq_in.rearrange("k (h d) -> k h d", h=H)
            split_lo(wqD[:, 1, :, 0, :], wq_v, wqD[:, 0, :, 0, :]).then_inc(s_wq, 1)
            split_latT(0)

            for slot in range(-KV_AHEAD, LAST_SLOT):
                b, p = divmod(slot, PAIRS)
                more = 0 <= b < NB - 1
                if slot + KV_AHEAD < NPAIR:
                    key_products(slot + KV_AHEAD)
                if more and p == 5:
                    split_ctxT(b + 1)
                second_layer(slot, "first")
                if slot == 0:
                    dve.wait_ge(s_const, 3)
                    nc.vector.tensor_copy(spread[:, :, :], spread_f[:, :, :]).then_inc(s_spread, 1)
                if 0 <= slot < NPAIR:
                    clip(slot, 0)
                side_taken(slot, "a")
                second_layer(slot, "early")
                if 0 <= slot + 1 < NPAIR:
                    query_lo(slot + 1)
                if more and p == 6:
                    split_latT(b + 1)
                if 0 <= slot + 1 < NPAIR:
                    key_lo(slot + 1)
                second_layer(slot, "mid")
                if 0 <= slot < NPAIR:
                    clip(slot, 1)
                second_layer(slot, "late")
                side_taken(slot, "b")
                if more:
                    if p == 1:
                        ctx_statistics(b + 1)
                        tokens_statistics(b + 1)
                    if p == 2:
                        ctx_normalise(b + 1)
                        tokens_normalise(b + 1)
                side_taken(slot, "c")
                second_layer(slot, "end")

        @block.gpsimd
        def _(pool):
            def own(ins):
                own.n += 1
                ins.then_inc(own_pool, 1)
                pool.wait_ge(own_pool, own.n)
            own.n = 0

            def inverse_root(dst, var, eps):
                own(nc.gpsimd.tensor_scalar_add(dst, var, eps))
                return nc.gpsimd.tensor_tensor(dst, dst, half_p[:, 0:dst.shape[1]], ALU.pow)

            def ctx_rstd(b):
                pool.wait_ge(s_cstat, b + 1)
                inverse_root(c_rstd[:, :], c_mv[:, :, 1], LN_EPS).then_inc(s_crstd, 1)

            def two_norms(rstd, both, mv, eps):
                own(inverse_root(rstd[:, :], mv[:, :, 1], LN_EPS))
                own(nc.gpsimd.tensor_tensor(both[:, :], rstd[:, :], rstd[:, :], ALU.mult))
                own(nc.gpsimd.tensor_tensor(both[:, :], both[:, :], mv[:, :, 1], ALU.mult))
                own(inverse_root(both[:, :], both[:, :], eps))
                return nc.gpsimd.tensor_tensor(both[:, :], both[:, :], rstd[:, :], ALU.mult)

            def tokens_rstd(b):
                pool.wait_ge(s_lstat, b + 1)
                two_norms(l_rstd, l2_rstd, l_mv, LN_EPS).then_inc(s_lrstd, 1)

            def mean_square_root(dst, ss):
                own(nc.gpsimd.tensor_scalar(dst[:, :], ss[:, :], 1.0 / D, RMS_EPS, ALU.mult, ALU.add))
                return nc.gpsimd.tensor_tensor(dst[:, :], dst[:, :], half_p[:, 0:TT], ALU.pow)

            nc.gpsimd.memset(half_p[:, :], -0.5)
            own(nc.gpsimd.memset(ident[:, :], 0.0))
            nc.gpsimd.affine_select(out=ident[:, :], in_=ident[:, :], compare_op=ALU.not_equal, fill=1.0, base=0,
                                    pattern=[[-1, 128]], channel_multiplier=1).then_inc(s_const, 1)
            ctx_rstd(0)
            tokens_rstd(0)
            pool.wait_ge(s_wqhi, 2)
            nc.gpsimd.tensor_tensor(wqD[:, 1, :, 1, :], wq_in.rearrange("k (h d) -> k h d", h=H), f(wqD[:, 0, :, 1, :]),
                                    ALU.subtract).then_inc(s_wq, 1)
            pool.wait_ge(s_wvhi, 1)
            nc.gpsimd.tensor_tensor(wvS[:, 1, :], wv_in, f(wvS[:, 0, :]), ALU.subtract).then_inc(s_wv, 1)
            own(nc.gpsimd.memset(sum_rows[:, :], 0.0))
            nc.gpsimd.memset(sum_rows[:, 24:32], 1.0).then_inc(s_const, 1)
            own(nc.gpsimd.memset(spread_f[:, :, :], 0.0))
            sp_v = spread_f[:, :, :].rearrange("k (i q) (h c) -> k i q h c", q=2, h=2)
            nc.gpsimd.affine_select(out=sp_v, in_=sp_v, compare_op=ALU.not_equal, fill=1.0, base=0,
                                    pattern=[[-8, PAIRS // 2], [-64, 2], [-32, 2], [0, DH]], channel_multiplier=1)\
                .then_inc(s_const, 1)

            def rotate(j):
                pool.wait_ge(s_kmul, 2 * j + 2)
                if j >= 2:
                    pool.wait_ge(s_klo, 2 * (j - 1))
                nc.gpsimd.tensor_tensor(krot[:, j % 2, :], kcos[:, j % 2, :], ksin[:, j % 2, :], ALU.add)\
                    .then_inc(s_krot, 1)

            def chunk_sums(j, h):
                n = 2 * j + h
                pool.wait_ge(s_clip, n + 1)
                if j >= 2 and h == 0:
                    pool.wait_ge(s_sum, j // 2)
                nc.gpsimd.tensor_tensor(esum[:, n % 4, :, :], e[:, n % 4, 0:2, :], e[:, n % 4, 2:4, :], ALU.add)\
                    .then_inc(s_esum, 1)

            def sum_experts(b, t):
                pool.wait_ge(*taken(f"moe{2 * t + 1}", b))
                pool.wait_ge(s_moe, 6 * (TT * b + t + 1))
                n = NE
                while n > 1:
                    n //= 2
                    own(nc.gpsimd.tensor_tensor(moe[:, t, 0:n, :], moe[:, t, 0:n, :], moe[:, t, n:2 * n, :], ALU.add))
                nc.gpsimd.tensor_tensor(x_in[:, TT * b + t, :], x_in[:, TT * b + t, :], moe[:, t, 0, :], ALU.add)\
                    .then_inc(s_y, 1)

            def second_layer(slot, part):
                for b in range(NB):
                    r = slot - PAIRS * (b + 1)
                    if (r, part) == (1, 0):
                        if b == 0:
                            pool.wait_ge(ld["bias"], 16 * 6)
                        pool.wait_ge(s_latn, b + 1)
                        tokens = x_in[:, TT * b:TT * b + TT, :]
                        nc.gpsimd.tensor_tensor(tokens, tokens, bo_r[:, :].unsqueeze(1).to_broadcast([128, TT, D]),
                                                ALU.add).then_inc(s_xb, 1)
                    if (r, part) == (2, 0):
                        pool.wait_ge(s_fstat, b + 1)
                        two_norms(f_rstd, rr1, f_mv, RMS_EPS).then_inc(s_frstd, 1)
                    if (r, part) == (3, 0):
                        pool.wait_ge(s_xl, b + 1)
                        nc.gpsimd.tensor_tensor(xl[:, b % 2, :, :], xl[:, b % 2, :, :],
                                                fbo_r[:, :].unsqueeze(1).to_broadcast([128, TT, D]), ALU.add)\
                            .then_inc(s_xlb, 1)
                    if r == 4:
                        if part == 0:
                            pool.wait_ge(*taken("keyval2", b))
                        last = products(nc.gpsimd, 1, part)
                        if part == 1:
                            last.then_inc(s_prod, 1)
                    if (r, part) in ((6, 1), (7, 0)):
                        if r == 6:
                            pool.wait_ge(s_atte, TT * b + 2)
                        last = weighted_values(nc.gpsimd, 1, r - 6)
                        if r == 7:
                            last.then_inc(s_prod2, 1)
                    if (r, part) == (9, 0):
                        pool.wait_ge(s_ss2, b + 1)
                        mean_square_root(rr2, ss2).then_inc(s_rr2, 1)
                        tokens = x_in[:, TT * b:TT * b + TT, :]
                        nc.gpsimd.tensor_tensor(tokens, tokens, xl[:, b % 2, :, :], ALU.add).then_inc(s_x23, 1)
                    if (r, part) in ((13, 1), (16, 0)) and b < NB - 1:
                        if r == 13:
                            pool.wait_ge(s_x23, b + 1)
                        sum_experts(b, part ^ 1)

            for slot in range(-KV_AHEAD, LAST_SLOT):
                b, p = divmod(slot, PAIRS)
                if slot + KV_AHEAD < NPAIR:
                    rotate(slot + KV_AHEAD)
                if 0 <= slot < NPAIR - 2:
                    chunk_sums(slot, 0)
                second_layer(slot, 0)
                if 0 <= slot < NPAIR - 2:
                    chunk_sums(slot, 1)
                second_layer(slot, 1)
                if 0 <= b < NB - 1:
                    if p == 1:
                        ctx_rstd(b + 1)
                        tokens_rstd(b + 1)


_INS = ['x', 'ctx_1024', 'L0_xattn_cos', 'L0_xattn_sin', 'L0_xattn_ln_lat_g', 'L0_xattn_ln_lat_b',
        'L0_xattn_ln_ctx_g', 'L0_xattn_ln_ctx_b', 'L0_xattn_Wq', 'L0_xattn_Wkv', 'L0_xattn_Wo', 'L0_xattn_bo',
        'L0_ffn_gamma1', 'L0_ffn_Wq', 'L0_ffn_bq', 'L0_ffn_Wdown', 'L0_ffn_bdown', 'L0_ffn_Wup', 'L0_ffn_bup',
        'L0_ffn_Wo', 'L0_ffn_bo', 'L0_ffn_gamma2', 'L0_ffn_Wg', 'L0_ffn_bg', 'L0_ffn_We']
_OUTS = [((4, 256, 128), 'float32')]


def kernel(**inputs):
    import numpy as _np
    import concourse.bacc as _bacc
    from concourse import mybir as _mybir
    from concourse.bass_utils import run_bass_kernel_spmd as _run

    nc = _bacc.Bacc("TRN2", target_bir_lowering=False, num_devices=1)
    arrays, args = {}, []
    for name in _INS:
        a = _np.ascontiguousarray(inputs[name])
        arrays[f"in_{name}_dram"] = a
        args.append(nc.dram_tensor(f"in_{name}_dram", a.shape, _mybir.dt.from_np(a.dtype), kind="ExternalInput").ap())
    for i, (shape, dtype) in enumerate(_OUTS):
        dt = _mybir.dt.from_np(_np.dtype(dtype))
        args.append(nc.dram_tensor(f"out_{i}_dram", shape, dt, kind="ExternalOutput").ap())
    xattn_ffn(nc, *args)
    r = _run(nc, [arrays], core_ids=[0])
    got = tuple(r.results[0][f"out_{i}_dram"] for i in range(len(_OUTS)))
    return got[0]
```

```python
import concourse.bass as bass
from concourse import mybir
from contextlib import ExitStack

fp32 = mybir.dt.float32
fp32r = mybir.dt.float32r
ALU = mybir.AluOpType
ACT = mybir.ActivationFunctionType
AX = mybir.AxisListType.X

NB = 4
NT = 256
NS = 512
D = 128
H = 16
DH = 64
HALF = DH // 2
INNER = H * DH
PAIRS = H // 2
NPAIR = NB * PAIRS
TT = NT // 128
SC = NS // 128
LN_EPS = 1e-5
RMS_EPS = 1e-6
SCALE = DH ** -0.5
EXP_LOW = 1.6701700790245659e-05
EXP_HIGH = 59874.141715197818
G = 16
GD = D // G
L = 64
NE = 8
SCALE2 = GD ** -0.5
KV_AHEAD = 2
LAST_SLOT = NPAIR + 2 * PAIRS + 1

POST_STEPS = {
    (1, "a"): "norm0", (1, "b"): "norm1", (1, "c"): "norm2", (2, "a"): "norm3", (2, "b"): "out_proj",
    (3, "c"): "h_T", (4, "a"): "query_down", (4, "b"): "keyval2", (8, "b"): "o_T", (8, "c"): "out_proj2",
    (10, "c"): "h2_T", (11, "a"): "gate", (13, "b"): "moe0", (13, "c"): "moe1", (15, "a"): "moe2",
    (16, "a"): "moe3",
}
LATE_STEPS = {
    (10, "c"): "o_T", (11, "b"): "out_proj2", (12, "c"): "h2_T", (13, "b"): "gate", (14, "b"): "moe0",
    (15, "b"): "moe1", (15, "c"): "moe2", (16, "a"): "moe3",
}
OWN_STEPS = {
    "reciprocals": [(0, "mid"), (0, "late"), (0, "end")],
    "statistics": [(2, "end"), (2, "end"), (2, "end")],
    "layer_norm": [(3, "first"), (3, "mid"), (3, "early")],
    "products_0": [(4, "end"), (4, "end"), (5, "mid")],
    "sum_0a": [(5, "mid"), (5, "early"), (6, "first")],
    "sum_0b": [(5, "late"), (5, "end"), (6, "first")],
    "sum_1a": [(6, "first"), (5, "end"), (6, "first")],
    "sum_1b": [(6, "early"), (6, "end"), (6, "mid")],
    "exp_0": [(5, "end"), (6, "end"), (5, "c")],
    "exp_1": [(6, "c"), (7, "c"), (5, "c")],
    "weigh_0a": [(6, "mid"), (7, "first"), (6, "late")],
    "weigh_0b": [(7, "mid"), (8, "late"), (6, "end")],
    "weigh_sum_1": [(7, "end"), (8, "early"), (8, "early")],
    "reduce_0": [(7, "mid"), (9, "first"), (7, "early")],
    "reduce_1": [(8, "early"), (10, "mid"), (8, "mid")],
    "root_norm": [(10, "first"), (12, "late"), (9, "early")],
    "gate_exps": [(11, None), (12, None), (16, None)],
    "gates": [(11, "late"), (14, "end"), (11, "late")],
    "add_bias": [(1, -1), (0, 1), (0, -1)],
    "two_norms": [(2, 0), (2, 0), (1, 0)],
    "xl_bias": [(4, -1), (3, -1), (2, 0)],
    "products_1a": [(4, 0), (4, 1), (4, 0)],
    "products_1b": [(5, -1), (5, -1), (4, 1)],
    "weigh_1a": [(6, -1), (6, 0), (5, 1)],
    "weigh_1b": [(6, -1), (8, 0), (6, 1)],
    "mean_square": [(9, 1), (10, -1), (6, 1)],
    "sum_experts_0": [(13, 1), (15, -1), (13, -1)],
    "sum_experts_1": [(16, -1), (15, -1), (13, 1)],
}
PREP_STEPS = {(4, "c"): "ctx_T", (6, "a"): "lat_T"}
WARM_UP = {"cos_T": 11, "ctx_T": 0, "sin_T": 4, "lat_T": 4}
FIRST_STEPS = [("cos_T", 0), ("ctx_T", 0), ("sin_T", 0), ("lat_T", 0)]


def stands(step, b, slot, place):
    return OWN_STEPS[step][max(0, b - (NB - 3))] == (slot - PAIRS * (b + 1), place)


def side_step(slot, pos):
    for b in range(NB):
        at = (slot - PAIRS * (b + 1), pos)
        name = POST_STEPS.get(at)
        if b == NB - 2 and (at[0] >= 8 or name in LATE_STEPS.values()):
            name = LATE_STEPS.get(at)
        if name:
            return name, b
        name = PREP_STEPS.get((slot - PAIRS * (b - 1), pos)) if b else None
        if name:
            return name, b
    return None


OTHER_BANKS = {
    ("cos_T", 0): 3, ("lat_T", 0): 3,
    ("moe1", NB - 2): 1, ("moe3", NB - 2): 1,
    ("norm0", NB - 1): 1, ("norm1", NB - 1): 2, ("norm2", NB - 1): 3, ("norm3", NB - 1): 4, ("out_proj", NB - 1): 5,
    ("h_T", NB - 1): 2, ("query_down", NB - 1): 3, ("keyval2", NB - 1): 4, ("o_T", NB - 1): 2,
    ("out_proj2", NB - 1): 3, ("h2_T", NB - 1): 4, ("gate", NB - 1): 5,
    ("moe0", NB - 1): 0, ("moe1", NB - 1): 1, ("moe2", NB - 1): 2, ("moe3", NB - 1): 3,
}
SIDE_BANKS = 6


def side_order():
    steps = list(FIRST_STEPS)
    for slot in range(-KV_AHEAD, LAST_SLOT):
        for pos in "abc":
            if side_step(slot, pos):
                steps.append(side_step(slot, pos))
    order, used = {}, [0] * SIDE_BANKS
    for step in steps:
        k = OTHER_BANKS.get(step, 0)
        order[step] = (k, used[k])
        used[k] += 1
    return order


SIDE = side_order()


def value_units(slot):
    b, p = divmod(slot, PAIRS)
    if p >= PAIRS - 2 and b + 1 < NB:
        first = 8 * (b + 1) + 2 * (p - (PAIRS - 2))
        return [first, first + 1]
    if 1 <= p <= 4 and 0 <= b < NB:
        return [8 * b + 3 + p]
    return []


def value_units_before(slot):
    return sum(len(value_units(s)) for s in range(-KV_AHEAD, slot))


def xattn_ffn(nc, x, ctx, cos, sin, ln_lat_g, ln_lat_b, ln_ctx_g, ln_ctx_b, Wq, Wkv, Wo, bo,
              gamma1, f_Wq, f_bq, f_Wdown, f_bdown, f_Wup, f_bup, f_Wo, f_bo, gamma2, f_Wg, f_bg, f_We, out):
    es = ExitStack()
    with es:
        def sb(name, shape, dt=fp32):
            return es.enter_context(nc.sbuf_tensor(name, shape, dt))

        def pb(name):
            return es.enter_context(nc.psum_tensor(name, [128, 512], fp32))

        def sem(name):
            return es.enter_context(nc.semaphore(name))

        x_in = sb("x_in", [128, NB * TT, D])
        ctx_in = sb("ctx_in", [128, 2, SC, D])
        cos_in = sb("cos_in", [128, SC, HALF])
        sin_in = sb("sin_in", [128, SC, HALF])
        prod = sb("prod", [128, TT, G * G * GD])
        wk_in, wv_in = (prod[:, 0, i * INNER:(i + 1) * INNER] for i in range(2))
        wq_in = prod[:, 1, 0:INNER]
        trig4 = prod[:, 1, INNER:2 * INNER].rearrange("p (w c r i) -> p w c r i", w=2, c=SC, r=4)
        cosT = sb("cosT", [128, NS])
        sinT = sb("sinT", [128, NS])
        vec = sb("vec", [128, 6])
        CTX_G, CTX_B, LAT_G, LAT_B, GAM1, GAM2 = (vec[:, i:i + 1] for i in range(6))
        bdown_c = sb("bdown_c", [L, 1])
        bo_r = sb("bo_r", [128, D])
        fbo_r = sb("fbo_r", [128, D])
        fbq_r = sb("fbq_r", [128, D])
        fbup_r = sb("fbup_r", [128, 2 * D])
        fbg_r = sb("fbg_r", [128, NE])
        ident = sb("ident", [128, 128])
        sum_rows = sb("sum_rows", [128, 56])
        spread = sb("spread", [128, PAIRS, 128], fp32r)
        wkA = sb("wkA", [128, 2, INNER], fp32r)
        wkB = sb("wkB", [128, 2, INNER], fp32r)
        wqD = sb("wqD", [128, 2, H, 2, DH], fp32r)
        wvS = sb("wvS", [128, 2, INNER], fp32r)
        wo = sb("wo", [128, PAIRS, D])
        fwq = sb("fwq", [128, D])
        fwdown = sb("fwdown", [128, L])
        fwup = sb("fwup", [L, 2 * D])
        fwo = sb("fwo", [128, D])
        fwg = sb("fwg", [128, NE])
        fwe = sb("fwe", [128, NE, D])
        c_stat = sb("c_stat", [128, SC, 6])
        c_mv = sb("c_mv", [128, SC, 2])
        c_rstd = sb("c_rstd", [128, SC])
        ctx_n = sb("ctx_n", [128, SC, D])
        l_stat = sb("l_stat", [128, TT, 6])
        l_mv = sb("l_mv", [128, TT, 2])
        l_rstd = sb("l_rstd", [128, TT])
        lat_2 = sb("lat_2", [128, TT, D])
        ctxT_f = sb("ctxT_f", [128, NS])
        latT_f = sb("latT_f", [128, NT])
        ctxT = sb("ctxT", [128, 2, NS], fp32r)
        latT = sb("latT", [128, 2, NT], fp32r)
        kcos = sb("kcos", [128, 2, NS])
        ksin = sb("ksin", [128, 2, NS])
        krot = sb("krot", [128, 2, NS])
        ks = sb("ks", [128, 3, 2, NS], fp32r)
        qs = sb("qs", [128, 2, 2, 2, NT], fp32r)
        v = sb("v", [128, SC, INNER])
        e = sb("e", [128, 4, SC, NT])
        esum = sb("esum", [128, 4, 2, NT])
        u = sb("u", [128, PAIRS, NT])
        spread_f = u[:, :, 0:128]
        on = sb("on", [128, PAIRS, NT])
        moe = on[:, :, :].rearrange("p g n -> p (g n)").rearrange("p (t e d) -> p t e d", t=TT, e=NE)
        rec = sb("rec", [128, NT])
        recS = sb("recS", [128, 2, NT], fp32r)
        f_stat = sb("f_stat", [128, TT, 6])
        f_mv = sb("f_mv", [128, TT, 2])
        f_rstd = sb("f_rstd", [128, TT])
        xl = sb("xl", [128, 2, TT, D])
        rr1 = sb("rr1", [128, TT])
        ss2 = sb("ss2", [128, TT])
        rr2 = sb("rr2", [128, TT])
        hn = sb("hn", [128, TT, D])
        hT = sb("hT", [128, NT])
        oT = sb("oT", [128, NT])
        hn2 = sb("hn2", [128, TT, D])
        q2 = sb("q2", [128, TT, D])
        dT = sb("dT", [L, NT])
        kv2 = sb("kv2", [128, TT, 2 * D])
        att = sb("att", [128, TT, G, G])
        amax = sb("amax", [128, TT, G])
        aden = sb("aden", [128, TT, G])
        o2 = sb("o2", [128, TT, D])
        h2T = sb("h2T", [128, NT])
        gl = sb("gl", [128, TT, NE])
        gmax = sb("gmax", [128, TT])
        gden = sb("gden", [128, TT])
        gate = sb("gate", [128, TT, NE])
        half_p = sb("half_p", [128, SC])

        sc_bank = [pb(f"sc{i}") for i in range(2)]
        pj_q = pb("pj_q")
        pj_k = [pb(f"pj_k{i}") for i in range(2)]
        pv_bank = pb("pv")
        sum_bank = pb("sums")
        first_value_banks = sc_bank + [pv_bank, sum_bank]
        side_banks = [pb("side")] + sc_bank + [pj_q] + pj_k

        ld = {n: sem(f"ld_{n}") for n in ("wk", "trig", "x", "wv", "wq", "bias", "wo", "ffn")}
        ld_ctx = [sem(f"ld_ctx{b}") for b in range(NB)]
        ld_vec = [sem(f"ld_vec{i}") for i in range(6)]
        s_const = sem("s_const")
        s_trig = sem("s_trig")
        s_wkhi = sem("s_wkhi")
        s_wqhi = sem("s_wqhi")
        s_wvhi = sem("s_wvhi")
        s_wk = sem("s_wk")
        s_wq = sem("s_wq")
        s_wv = sem("s_wv")
        s_spread = sem("s_spread")
        s_cstat = sem("s_cstat")
        s_crstd = sem("s_crstd")
        s_ctxn = sem("s_ctxn")
        s_lstat = sem("s_lstat")
        s_lrstd = sem("s_lrstd")
        s_latn = sem("s_latn")
        s_ctxT = sem("s_ctxT")
        s_latT = sem("s_latT")
        s_side = [sem(f"s_side{k}") for k in range(SIDE_BANKS)]
        s_side_free = [sem(f"s_side_free{k}") for k in range(SIDE_BANKS)]
        s_kproj = sem("s_kproj")
        s_kmul = sem("s_kmul")
        s_krot = sem("s_krot")
        s_khi = sem("s_khi")
        s_klo = sem("s_klo")
        s_qproj = sem("s_qproj")
        s_qhi = sem("s_qhi")
        s_qlo = sem("s_qlo")
        s_vproj = sem("s_vproj")
        s_v = sem("s_v")
        s_score = sem("s_score")
        s_exp = sem("s_exp")
        s_clip = sem("s_clip")
        s_esum = sem("s_esum")
        s_pv = sem("s_pv")
        s_sum = sem("s_sum")
        s_u = sem("s_u")
        s_rec = sem("s_rec")
        s_recS = sem("s_recS")
        s_xb = sem("s_xb")
        s_fstat = sem("s_fstat")
        s_rr1 = sem("s_rr1")
        s_frstd = sem("s_frstd")
        s_xl = sem("s_xl")
        s_hn = sem("s_hn")
        s_xlb = sem("s_xlb")
        s_dT = sem("s_dT")
        s_prod = sem("s_prod")
        s_attm = sem("s_attm")
        s_atte = sem("s_atte")
        s_prod2 = sem("s_prod2")
        s_o2 = sem("s_o2")
        s_ss2 = sem("s_ss2")
        s_rr2 = sem("s_rr2")
        s_hn2 = sem("s_hn2")
        s_x23 = sem("s_x23")
        s_mix = sem("s_mix")
        s_glm = sem("s_glm")
        s_gle = sem("s_gle")
        s_gate = sem("s_gate")
        s_moe = sem("s_moe")
        s_y = sem("s_y")
        s_out = sem("s_out")
        own_dve = sem("own_dve")
        own_act = sem("own_act")
        own_pool = sem("own_pool")

        def f(ap):
            return ap.bitcast(fp32)

        block = es.enter_context(nc.Block())

        def made(name, b):
            k, n = SIDE[name, b]
            return s_side[k], n + 1

        def taken(name, b):
            k, n = SIDE[name, b]
            return s_side_free[k], n + 1

        def value_bank(n):
            return first_value_banks[n] if n < len(first_value_banks) else pj_k[n % 2]

        @block.sync
        def _(sp):
            x_v = x.rearrange("b (t p) d -> p (b t) d", p=128)
            ctx_v = ctx.rearrange("b (c p) d -> p (b c) d", p=128)
            out_v = out.rearrange("b (t p) d -> b p t d", p=128)
            def load_ctx(b):
                if b >= 2:
                    sp.wait_ge(s_ctxn, b - 1)
                sp.dma_start(ctx_in[:, b % 2, :, :], ctx_v[:, SC * b:SC * b + SC, :]).then_inc(ld_ctx[b], 16)

            def load_vec(columns):
                for i in columns:
                    col = (ln_ctx_g, ln_ctx_b, ln_lat_g, ln_lat_b, gamma1, gamma2)[i]
                    sp.dma_start(vec[:, i:i + 1], col.rearrange("(p a) -> p a", a=1)).then_inc(ld_vec[i], 16)

            load_ctx(0)
            sp.dma_start(wk_in, Wkv[:, 0:INNER]).then_inc(ld["wk"], 16)
            load_vec((0, 1))
            sp.dma_start(x_in[:, :, :], x_v).then_inc(ld["x"], 16)
            sp.dma_start(wq_in, Wq).then_inc(ld["wq"], 16)
            sp.dma_start(wv_in, Wkv[:, INNER:2 * INNER]).then_inc(ld["wv"], 16)
            load_vec((2, 3, 4, 5))
            load_ctx(1)
            sp.dma_start(wo[:, :, :], Wo.rearrange("(g p) n -> p g n", p=128)).then_inc(ld["wo"], 16)
            for dst, src in ((fwq[:, :], f_Wq), (fwdown[:, :], f_Wdown), (fwup[:, :], f_Wup), (fwo[:, :], f_Wo),
                             (fwg[:, :], f_Wg), (fwe[:, :, :], f_We.rearrange("e d f -> d e f"))):
                sp.dma_start(dst, src).then_inc(ld["ffn"], 16)
            sp.dma_start(bdown_c[:, :], f_bdown.rearrange("(p a) -> p a", a=1)).then_inc(ld["bias"], 16)
            for dst, row in ((bo_r, bo), (fbo_r, f_bo), (fbq_r, f_bq), (fbup_r, f_bup), (fbg_r, f_bg)):
                sp.dma_start(dst[:, :], row.rearrange("(a n) -> a n", a=1).to_broadcast([128, row.shape[0]]))\
                    .then_inc(ld["bias"], 16)
            for b in range(2, NB):
                load_ctx(b)
            for b in range(NB):
                if b < NB - 1:
                    sp.wait_ge(s_y, TT * (b + 1))
                else:
                    sp.wait_ge(s_mix, TT * NE)
                sp.dma_start(out_v[b], x_in[:, TT * b:TT * b + TT, :]).then_inc(s_out, 16)
            sp.wait_ge(s_out, 16 * NB)

        @block.tensor
        def _(pe):
            def split3(out_ap, w_hi, w_lo, m_hi, m_lo):
                nc.tensor.matmul(out_ap, w_hi, m_hi, start=True, stop=False)
                nc.tensor.matmul(out_ap, w_hi, m_lo, start=False, stop=False)
                return nc.tensor.matmul(out_ap, w_lo, m_hi, start=False, stop=True)

            def keys(j):
                b, p = divmod(j, PAIRS)
                cols = slice(128 * p, 128 * p + 128)
                if p == 0:
                    pe.wait_ge(s_ctxT, b + 1)
                if j == 0:
                    pe.wait_ge(s_wk, 1)
                done = value_units_before(j - KV_AHEAD)
                if done > len(first_value_banks):
                    pe.wait_ge(s_v, done)
                if j:
                    pe.wait_ge(s_kmul, 2 * j)
                split3(pj_k[0][:, :], wkA[:, 0, cols], wkA[:, 1, cols], ctxT[:, 0, :], ctxT[:, 1, :]).then_inc(s_kproj, 1)
                if j == 0:
                    pe.wait_ge(s_wk, 2)
                split3(pj_k[1][:, :], wkB[:, 0, cols], wkB[:, 1, cols], ctxT[:, 0, :], ctxT[:, 1, :]).then_inc(s_kproj, 1)

            def queries(j):
                b, p = divmod(j, PAIRS)
                if p == 0:
                    pe.wait_ge(s_latT, b + 1)
                if j == 0:
                    pe.wait_ge(s_wq, 1)
                if j:
                    pe.wait_ge(s_qlo, j)
                for h in range(2):
                    w = wqD[:, :, 2 * p + h, :, :].rearrange("k s t d -> k s (t d)")
                    last = split3(pj_q[:, h * NT:(h + 1) * NT], w[:, 0, :], w[:, 1, :], latT[:, 0, :], latT[:, 1, :])
                last.then_inc(s_qproj, 1)

            def values(n, slot):
                b, unit = divmod(n, 8)
                half, c = divmod(unit, SC)
                if n == 0:
                    pe.wait_ge(s_wv, 1)
                if n >= len(first_value_banks):
                    pe.wait_ge(s_v, n - 1)
                    pe.wait_ge(s_kmul, 2 * min(slot + KV_AHEAD + 1, NPAIR))
                rows = slice(128 * c, 128 * c + 128)
                cols = slice(512 * half, 512 * half + 512)
                split3(value_bank(n)[:, :], ctxT[:, 0, rows], ctxT[:, 1, rows], wvS[:, 0, cols], wvS[:, 1, cols])\
                    .then_inc(s_vproj, 1)

            def scores(j, h):
                if h == 0:
                    pe.wait_ge(s_klo, 2 * j + 2)
                    pe.wait_ge(s_qlo, j + 1)
                for half in range(2):
                    n = 4 * j + 2 * h + half
                    if n < 2:
                        pe.wait_ge(s_v, n + 1)
                    if n >= 2:
                        pe.wait_ge(s_exp, n - 1)
                    for c in range(2):
                        dst = sc_bank[n % 2][:, c * NT:(c + 1) * NT]
                        w = ks[:, j % 3, h, 128 * (2 * half + c):128 * (2 * half + c) + 128]
                        nc.tensor.matmul(dst, w, qs[:, j % 2, 0, h, :], start=True, stop=False)
                        last = nc.tensor.matmul(dst, w, qs[:, j % 2, 1, h, :], start=False, stop=True)
                    last.then_inc(s_score, 1)

            def times_values(j):
                b, p = divmod(j, PAIRS)
                pe.wait_ge(s_clip, 2 * j + 2)
                pe.wait_ge(s_v, 8 * b + (4 if p < PAIRS // 2 else 8))
                if j:
                    pe.wait_ge(s_u, j)
                for c in range(SC):
                    for h in range(2):
                        col = 128 * p + DH * h
                        last = nc.tensor.matmul(pv_bank[DH * h:DH * h + DH, 0:NT], v[:, c, col:col + DH],
                                                e[:, (2 * j + h) % 4, c, :], start=(c == 0), stop=(c == SC - 1))
                last.then_inc(s_pv, 1)

            def sums(j):
                b, p = divmod(j, PAIRS)
                if j < NPAIR - 1:
                    pe.wait_ge(s_esum, 2 * j + 2)
                    source, chunks = esum, 2
                else:
                    pe.wait_ge(s_clip, 2 * j + 2)
                    source, chunks = e, SC
                if p == 1 and b:
                    pe.wait_ge(s_rec, b)
                if j == 1:
                    pe.wait_ge(s_const, 2)
                    pe.wait_ge(s_v, 4)
                w = sum_rows[:, 24 - 8 * (p // 2):56 - 8 * (p // 2)]
                for c in range(chunks):
                    for g in range(4):
                        last = nc.tensor.matmul(sum_bank[32 * g:32 * g + 32, 0:NT], w,
                                                source[:, (2 * (j - 1) + g) % 4, c, :],
                                                start=(p == 1 and c == 0), stop=(p == PAIRS - 1 and c == chunks - 1))
                last.then_inc(s_sum, 1)

            def transposes(side, tiles):
                for t, tile in enumerate(tiles):
                    last = nc.tensor.transpose(side[:, 128 * t:128 * t + 128], tile, ident[:, :])
                return last

            def side_product(name, b):
                k, n = SIDE[name, b]
                side = side_banks[k]
                source = {"query_down": "h_T", "out_proj2": "o_T",
                          "gate": "h2_T"}.get(name)
                if source:
                    pe.wait_ge(*taken(source, b))
                if n:
                    pe.wait_ge(s_side_free[k], n)
                if (name, b) in FIRST_STEPS:
                    pass
                elif 1 <= k <= 2:
                    pe.wait_ge(s_exp, 4 * NPAIR)
                elif k == 3:
                    pe.wait_ge(s_qlo, NPAIR)
                elif k >= 4:
                    pe.wait_ge(s_kmul, 2 * NPAIR)
                    pe.wait_ge(s_v, 8 * NB)
                if name == "ctx_T":
                    pe.wait_ge(s_ctxn, b + 1)
                    last = transposes(side, [ctx_n[:, c, :] for c in range(SC)])
                elif name in ("cos_T", "sin_T"):
                    which = int(name == "sin_T")
                    pe.wait_ge(s_const, 1)
                    pe.wait_ge(s_trig, 4 * (which + 1))
                    last = transposes(side, [trig4[:, which, c, :, :].rearrange("p r i -> p (r i)") for c in range(SC)])
                elif name == "lat_T":
                    pe.wait_ge(s_latn, b + 1)
                    last = transposes(side, [lat_2[:, t, :] for t in range(TT)])
                elif name.startswith("norm"):
                    if name == "norm0":
                        pe.wait_ge(s_recS, b + 1)
                    if name == "norm0" and b == 0:
                        pe.wait_ge(s_spread, 1)
                    for i in range(2):
                        p = 2 * int(name[4]) + i
                        dst = side[:, i * NT:(i + 1) * NT]
                        nc.tensor.matmul(dst, spread[:, p, :], recS[:, 0, :], start=True, stop=False)
                        last = nc.tensor.matmul(dst, spread[:, p, :], recS[:, 1, :], start=False, stop=True)
                elif name == "out_proj":
                    if b == 0:
                        pe.wait_ge(ld["wo"], 16)
                    for t in range(TT):
                        for p in range(PAIRS):
                            if t == 0 and p % 2 == 0:
                                pe.wait_ge(*taken(f"norm{p // 2}", b))
                            last = nc.tensor.matmul(side[:, t * D:(t + 1) * D], on[:, p, 128 * t:128 * t + 128],
                                                    wo[:, p, :], start=(p == 0), stop=(p == PAIRS - 1))
                elif name == "h_T":
                    pe.wait_ge(s_hn, b + 1)
                    last = transposes(side, [hn[:, t, :] for t in range(TT)])
                elif name == "query_down":
                    if b == 0:
                        pe.wait_ge(ld["ffn"], 16 * 6)
                    for t in range(TT):
                        nc.tensor.matmul(side[:, t * D:(t + 1) * D], hT[:, 128 * t:128 * t + 128], fwq[:, :],
                                         start=True, stop=True)
                    last = nc.tensor.matmul(side[0:L, NT:2 * NT], fwdown[:, :], hT[:, :], start=True, stop=True)
                elif name == "keyval2":
                    pe.wait_ge(s_dT, b + 1)
                    for t in range(TT):
                        last = nc.tensor.matmul(side[:, 2 * D * t:2 * D * (t + 1)], dT[:, 128 * t:128 * t + 128],
                                                fwup[:, :], start=True, stop=True)
                elif name == "o_T":
                    pe.wait_ge(s_o2, b + 1)
                    last = transposes(side, [o2[:, t, :] for t in range(TT)])
                elif name == "out_proj2":
                    for t in range(TT):
                        last = nc.tensor.matmul(side[:, t * D:(t + 1) * D], oT[:, 128 * t:128 * t + 128], fwo[:, :],
                                                start=True, stop=True)
                elif name == "h2_T":
                    pe.wait_ge(s_hn2, b + 1)
                    last = transposes(side, [hn2[:, t, :] for t in range(TT)])
                elif name == "gate":
                    for t in range(TT):
                        last = nc.tensor.matmul(side[:, t * NE:(t + 1) * NE], h2T[:, 128 * t:128 * t + 128], fwg[:, :],
                                                start=True, stop=True)
                elif name.startswith("moe"):
                    t, half = divmod(int(name[3]), 2)
                    w = fwe[:, 4 * half:4 * half + 4, :].rearrange("d e f -> d (e f)")
                    last = nc.tensor.matmul(side[:, :], h2T[:, 128 * t:128 * t + 128], w, start=True, stop=True)
                last.then_inc(s_side[k], 1)

            def side_at(slot, pos):
                step = side_step(slot, pos)
                if step:
                    side_product(*step)

            pe.wait_ge(s_const, 1)
            for name, b in FIRST_STEPS:
                for _ in range(WARM_UP[name]):
                    nc.tensor.matmul(pv_bank[:, 0:128], ident[:, :], ident[:, :], start=True, stop=True)
                side_product(name, b)
            for slot in range(-KV_AHEAD, LAST_SLOT):
                if slot + KV_AHEAD < NPAIR:
                    keys(slot + KV_AHEAD)
                if 0 <= slot < NPAIR:
                    scores(slot, 0)
                side_at(slot, "a")
                if 0 <= slot + 1 < NPAIR:
                    queries(slot + 1)
                if 2 <= slot <= NPAIR and slot % 2 == 0:
                    sums(slot - 1)
                if 0 <= slot < NPAIR:
                    scores(slot, 1)
                for n in value_units(slot):
                    values(n, slot)
                side_at(slot, "b")
                if 1 <= slot <= NPAIR:
                    times_values(slot - 1)
                side_at(slot, "c")

        @block.scalar
        def _(act):
            def own(ins):
                own.n += 1
                ins.then_inc(own_act, 1)
                act.wait_ge(own_act, own.n)
            own.n = 0

            act.dma_start(cos_in[:, :, :], cos.rearrange("(c p) i -> p c i", p=128)).then_inc(ld["trig"], 16)
            act.dma_start(sin_in[:, :, :], sin.rearrange("(c p) i -> p c i", p=128)).then_inc(ld["trig"], 16)
            act.preload_act_table(ACT.Exp)

            def key_hi(j):
                act.wait_ge(s_krot, j + 1)
                if j >= 3:
                    act.wait_ge(s_score, 4 * (j - 3) + 4)
                for h in range(2):
                    rows = slice(DH * h, DH * h + DH)
                    nc.scalar.activation(ks[rows, j % 3, h, :], krot[rows, j % 2, :], ACT.Copy).then_inc(s_khi, 1)

            def query_hi(j):
                act.wait_ge(s_qproj, j + 1)
                if j >= 2:
                    act.wait_ge(s_score, 4 * (j - 2) + 4)
                nc.scalar.activation(qs[:, j % 2, 0, :, :].rearrange("p h n -> p (h n)"), pj_q[:, :], ACT.Copy)\
                    .then_inc(s_qhi, 1)

            def value_copy(n):
                b, unit = divmod(n, 8)
                half, c = divmod(unit, SC)
                act.wait_ge(s_vproj, n + 1)
                if b:
                    act.wait_ge(s_pv, PAIRS * (b - 1) + (PAIRS // 2 if half == 0 else PAIRS))
                nc.scalar.activation(v[:, c, 512 * half:512 * half + 512], value_bank(n)[:, :], ACT.Copy).then_inc(s_v, 1)

            def exps(j, h):
                for half in range(2):
                    n = 4 * j + 2 * h + half
                    act.wait_ge(s_score, n + 1)
                    if j >= 2 and h == 0 and half == 0:
                        act.wait_ge(s_pv, j - 1)
                        act.wait_ge(s_esum, 2 * (j - 1))
                    nc.scalar.activation(e[:, (2 * j + h) % 4, 2 * half:2 * half + 2, :].rearrange("p c n -> p (c n)"),
                                         sc_bank[n % 2][:, :], ACT.Exp, scale=SCALE).then_inc(s_exp, 1)

            def attention_copy(j):
                act.wait_ge(s_pv, j + 1)
                if j >= PAIRS:
                    act.wait_ge(*taken(f"norm{j % PAIRS // 2}", j // PAIRS - 1))
                nc.scalar.activation(u[:, j % PAIRS, :], pv_bank[:, 0:NT], ACT.Copy).then_inc(s_u, 1)

            def side_taken(slot, pos):
                step = side_step(slot, pos)
                if step:
                    take(*step)

            def take(name, b):
                k = SIDE[name, b][0]
                side, free = side_banks[k], s_side_free[k]
                if name == "ctx_T":
                    act.wait_ge(*made(name, b))
                    if b == 0:
                        act.wait_ge(ld_vec[0], 16)
                        act.wait_ge(ld_vec[1], 16)
                    else:
                        act.wait_ge(s_ctxT, b)
                    nc.scalar.activation(ctxT_f[:, :], side[:, :], ACT.Identity, scale=CTX_G, bias=CTX_B)\
                        .then_inc(free, 1)
                elif name in ("cos_T", "sin_T"):
                    act.wait_ge(*made(name, b))
                    dst = cosT if name == "cos_T" else sinT
                    nc.scalar.activation(dst[:, :], side[:, :], ACT.Copy).then_inc(free, 1)
                elif name == "lat_T":
                    act.wait_ge(*made(name, b))
                    if b == 0:
                        act.wait_ge(ld_vec[2], 16)
                        act.wait_ge(ld_vec[3], 16)
                    else:
                        act.wait_ge(s_latT, b)
                    nc.scalar.activation(latT_f[:, :], side[:, 0:NT], ACT.Identity, scale=LAT_G, bias=LAT_B)\
                        .then_inc(free, 1)
                elif name == "h_T":
                    if b == 0:
                        act.wait_ge(ld_vec[4], 16)
                    act.wait_ge(*made(name, b))
                    nc.scalar.activation(hT[:, :], side[:, 0:NT], ACT.Copy, scale=GAM1).then_inc(free, 1)
                elif name == "query_down":
                    if b == 0:
                        act.wait_ge(ld["bias"], 16 * 6)
                    act.wait_ge(*made(name, b))
                    nc.scalar.activation(dT[:, :], side[0:L, NT:2 * NT], ACT.Identity, bias=bdown_c[:, :])\
                        .then_inc(s_dT, 1)
                elif name == "o_T":
                    act.wait_ge(*made(name, b))
                    nc.scalar.activation(oT[:, :], side[:, 0:NT], ACT.Copy).then_inc(free, 1)
                elif name == "h2_T":
                    if b == 0:
                        act.wait_ge(ld_vec[5], 16)
                    act.wait_ge(*made(name, b))
                    nc.scalar.activation(h2T[:, :], side[:, 0:NT], ACT.Copy, scale=GAM2).then_inc(free, 1)
                elif name.startswith("moe") and b < NB - 1:
                    t, half = divmod(int(name[3]), 2)
                    if name == "moe0":
                        act.wait_ge(s_gate, b + 1)
                    if half == 0 and b:
                        act.wait_ge(s_y, TT * (b - 1) + t + 1)
                    act.wait_ge(*made(name, b))
                    for i in range(4):
                        last = nc.scalar.activation(moe[:, t, 4 * half + i, :], side[:, D * i:D * i + D], ACT.Copy,
                                                    scale=gate[:, t, 4 * half + i:4 * half + i + 1])
                        last.then_inc(free if i == 3 else s_moe, 1)

            act.wait_ge(ld["wk"], 16)
            nc.scalar.activation(wkA[:, 0, :], wk_in, ACT.Copy).then_inc(s_wkhi, 1)
            take("cos_T", 0)
            take("ctx_T", 0)
            act.wait_ge(ld["wq"], 16)
            wq_twice = wq_in.rearrange("k (h d) -> k h d", h=H)
            for t in range(2):
                nc.scalar.activation(wqD[:, 0, :, t, :], wq_twice, ACT.Copy).then_inc(s_wqhi, 1)
            take("sin_T", 0)
            act.wait_ge(ld["wv"], 16)
            nc.scalar.activation(wvS[:, 0, :], wv_in, ACT.Copy).then_inc(s_wvhi, 1)
            take("lat_T", 0)

            def second_layer(slot, place):
                for b in range(NB):
                    for t in range(TT):
                        if not stands(f"exp_{t}", b, slot, place):
                            continue
                        act.wait_ge(s_attm, TT * b + t + 1)
                        a = att[:, t, :, :].rearrange("p h g -> p (h g)")
                        nc.scalar.activation(a, a, ACT.Exp, scale=SCALE2).then_inc(s_atte, 1)

            def gate_exps(slot):
                for b in range(NB):
                    if stands("gate_exps", b, slot, None):
                        act.wait_ge(s_glm, b + 1)
                        a = gl[:, :, :].rearrange("p t n -> p (t n)")
                        nc.scalar.activation(a, a, ACT.Exp).then_inc(s_gle, 1)

            for slot in range(-KV_AHEAD, LAST_SLOT):
                if 0 <= slot < NPAIR:
                    exps(slot, 0)
                side_taken(slot, "a")
                if 0 <= slot + 1 < NPAIR:
                    query_hi(slot + 1)
                if 0 <= slot < NPAIR:
                    exps(slot, 1)
                for n in value_units(slot):
                    value_copy(n)
                if slot + KV_AHEAD < NPAIR:
                    key_hi(slot + KV_AHEAD)
                side_taken(slot, "b")
                if 1 <= slot <= NPAIR:
                    attention_copy(slot - 1)
                second_layer(slot, "c")
                side_taken(slot, "c")
                second_layer(slot, "end")
                gate_exps(slot)

        def products(engine, t, hh):
            q_v = q2[:, t, :].rearrange("p (h d) -> p h d", h=G)[:, 8 * hh:8 * hh + 8, :]
            k_v = kv2[:, t, :].rearrange("p (g c) -> p g c", g=G)[:, :, 0:GD]
            return engine.tensor_tensor(
                prod[:, t, 1024 * hh:1024 * hh + 1024].rearrange("p (h g d) -> p h g d", h=G // 2, g=G),
                q_v.unsqueeze(2).to_broadcast([128, G // 2, G, GD]),
                k_v.unsqueeze(1).to_broadcast([128, G // 2, G, GD]), ALU.mult)

        def weighted_values(engine, t, hh):
            v_v = kv2[:, t, :].rearrange("p (g c) -> p c g", g=G)[:, GD:2 * GD, :]
            return engine.tensor_tensor(
                prod[:, t, 1024 * hh:1024 * hh + 1024].rearrange("p (h d g) -> p h d g", h=G // 2, d=GD),
                att[:, t, 8 * hh:8 * hh + 8, :].unsqueeze(2).to_broadcast([128, G // 2, GD, G]),
                v_v.unsqueeze(1).to_broadcast([128, G // 2, GD, G]), ALU.mult)

        @block.vector
        def _(dve):
            def own(ins):
                own.n += 1
                ins.then_inc(own_dve, 1)
                dve.wait_ge(own_dve, own.n)
            own.n = 0

            def split_lo(dst, whole, hi):
                return nc.vector.tensor_tensor(dst, whole, f(hi), ALU.subtract)

            def statistics(mv, stat, tiles):
                for t, tile in enumerate(tiles):
                    last = nc.vector.bn_stats(stat[:, t, :], tile)
                own(last)
                for t in range(len(tiles)):
                    last = nc.vector.bn_aggr(mv[:, t, :], stat[:, t, :])
                return last

            def normalise(dst, src, mv, rstd, n):
                for t in range(n):
                    last = nc.vector.tensor_scalar(dst[:, t, :], src[:, t, :], mv[:, t, 0:1], rstd[:, t:t + 1],
                                                   ALU.subtract, ALU.mult)
                return last

            def ctx_statistics(b):
                dve.wait_ge(ld_ctx[b], 16)
                statistics(c_mv, c_stat, [ctx_in[:, b % 2, c, :] for c in range(SC)]).then_inc(s_cstat, 1)

            def ctx_normalise(b):
                dve.wait_ge(s_crstd, b + 1)
                if b:
                    dve.wait_ge(*made("ctx_T", b - 1))
                normalise(ctx_n, ctx_in[:, b % 2, :, :], c_mv, c_rstd, SC).then_inc(s_ctxn, 1)

            def tokens_statistics(b):
                if b == 0:
                    dve.wait_ge(ld["x"], 16)
                statistics(l_mv, l_stat, [x_in[:, TT * b + t, :] for t in range(TT)]).then_inc(s_lstat, 1)

            def tokens_normalise(b):
                dve.wait_ge(s_lrstd, b + 1)
                if b:
                    dve.wait_ge(*made("lat_T", b - 1))
                normalise(lat_2, x_in[:, TT * b:TT * b + TT, :], l_mv, l_rstd, TT).then_inc(s_latn, 1)

            def split_ctxT(b):
                dve.wait_ge(*taken("ctx_T", b))
                if b:
                    dve.wait_ge(s_kproj, 2 * PAIRS * b)
                    dve.wait_ge(s_vproj, 8 * b)
                own(nc.vector.tensor_copy(ctxT[:, 0, :], ctxT_f[:, :]))
                split_lo(ctxT[:, 1, :], ctxT_f[:, :], ctxT[:, 0, :]).then_inc(s_ctxT, 1)

            def split_latT(b):
                dve.wait_ge(*taken("lat_T", b))
                if b:
                    dve.wait_ge(s_qproj, PAIRS * b)
                own(nc.vector.tensor_copy(latT[:, 0, :], latT_f[:, :]))
                split_lo(latT[:, 1, :], latT_f[:, :], latT[:, 0, :]).then_inc(s_latT, 1)

            def key_products(j):
                if j == 0:
                    dve.wait_ge(*taken("sin_T", 0))
                if j >= 2:
                    dve.wait_ge(s_krot, j - 1)
                for i, (dst, bank, trig) in enumerate(((kcos, pj_k[0], cosT), (ksin, pj_k[1], sinT))):
                    dve.wait_ge(s_kproj, 2 * j + i + 1)
                    nc.vector.tensor_tensor(dst[:, j % 2, :], bank[:, :], trig[:, :], ALU.mult).then_inc(s_kmul, 1)

            def key_lo(j):
                for h in range(2):
                    dve.wait_ge(s_khi, 2 * j + h + 1)
                    own_rows = slice(DH * h, DH * h + DH)
                    other = slice(DH * (1 - h), DH * (1 - h) + DH)
                    split_lo(ks[other, j % 3, h, :], krot[own_rows, j % 2, :], ks[own_rows, j % 3, h, :])\
                        .then_inc(s_klo, 1)

            def query_lo(j):
                dve.wait_ge(s_qhi, j + 1)
                split_lo(qs[:, j % 2, 1, :, :].rearrange("p h n -> p (h n)"), pj_q[:, :],
                         qs[:, j % 2, 0, :, :].rearrange("p h n -> p (h n)")).then_inc(s_qlo, 1)

            def clip(j, h):
                dve.wait_ge(s_exp, 4 * j + 2 * h + 2)
                a = e[:, (2 * j + h) % 4, :, :].rearrange("p c n -> p (c n)")
                nc.vector.tensor_scalar(a, a, EXP_LOW, EXP_HIGH, ALU.max, ALU.min).then_inc(s_clip, 1)

            def reciprocals(b):
                dve.wait_ge(s_sum, PAIRS // 2 * (b + 1))
                nc.vector.reciprocal(rec[:, :], sum_bank[:, 0:NT]).then_inc(s_rec, 1)
                dve.wait_ge(s_rec, b + 1)
                own(nc.vector.tensor_copy(recS[:, 0, :], rec[:, :]))
                split_lo(recS[:, 1, :], rec[:, :], recS[:, 0, :]).then_inc(s_recS, 1)

            def tokens(b):
                return x_in[:, TT * b:TT * b + TT, :]

            def side_taken(slot, pos):
                step = side_step(slot, pos)
                if step and step[0] != "out_proj":
                    take(*step)

            def flat(ap):
                return ap.rearrange("p t n -> p (t n)")

            def twice(row):
                return row[:, :].unsqueeze(1).to_broadcast([128, TT, row.shape[1]])

            def square_sums(ss, src):
                for t in range(TT):
                    last = nc.vector.tensor_tensor_reduce(out=hn2[:, t, :], in0=src[:, t, :], in1=src[:, t, :], scale=1.0,
                                                          scalar=0.0, op0=ALU.mult, op1=ALU.add,
                                                          accum_out=ss[:, t:t + 1])
                return last

            def take(name, b):
                k = SIDE[name, b][0]
                side, free = side_banks[k], s_side_free[k]
                if name.startswith("norm"):
                    i = int(name[4])
                    dve.wait_ge(s_u, PAIRS * b + 2 * i + 2)
                    if i == 0 and b:
                        dve.wait_ge(*made("out_proj", b - 1))
                    if i == 0 and b >= 2:
                        dve.wait_ge(s_y, TT * (b - 1))
                    dve.wait_ge(*made(name, b))
                    nc.vector.tensor_tensor(flat(on[:, 2 * i:2 * i + 2, :]), flat(u[:, 2 * i:2 * i + 2, :]),
                                            side[:, :], ALU.mult).then_inc(free, 1)
                elif name == "out_proj":
                    dve.wait_ge(s_xb, b + 1)
                    dve.wait_ge(*made(name, b))
                    nc.vector.tensor_tensor(flat(tokens(b)), side[:, 0:NT], flat(tokens(b)), ALU.add)\
                        .then_inc(free, 1)
                elif name == "query_down":
                    if b == 0:
                        dve.wait_ge(ld["bias"], 16 * 6)
                    if b:
                        dve.wait_ge(s_prod, b)
                    dve.wait_ge(s_dT, b + 1)
                    nc.vector.tensor_tensor(q2[:, :, :], side[:, 0:NT].rearrange("p (t n) -> p t n", t=TT),
                                            twice(fbq_r), ALU.add).then_inc(free, 1)
                elif name == "keyval2":
                    if b:
                        dve.wait_ge(s_prod2, b)
                    dve.wait_ge(*made(name, b))
                    nc.vector.tensor_tensor(kv2[:, :, :], side[:, :].rearrange("p (t n) -> p t n", t=TT),
                                            twice(fbup_r), ALU.add).then_inc(free, 1)
                    dve.wait_ge(*taken(name, b))
                elif name == "out_proj2":
                    dve.wait_ge(s_xlb, b + 1)
                    dve.wait_ge(*made(name, b))
                    nc.vector.tensor_tensor(flat(xl[:, b % 2, :, :]), side[:, 0:NT], flat(xl[:, b % 2, :, :]), ALU.add)\
                        .then_inc(free, 1)
                    dve.wait_ge(*taken(name, b))
                    square_sums(ss2, xl[:, b % 2, :, :]).then_inc(s_ss2, 1)
                elif name == "gate":
                    dve.wait_ge(*made(name, b))
                    nc.vector.tensor_tensor(gl[:, :, :], side[:, 0:TT * NE].rearrange("p (t n) -> p t n", t=TT),
                                            twice(fbg_r), ALU.add).then_inc(free, 1)
                    dve.wait_ge(*taken(name, b))
                    own(nc.vector.tensor_reduce(gmax[:, :], gl[:, :, :], AX, ALU.max))
                    nc.vector.tensor_tensor(gl[:, :, :], gl[:, :, :],
                                            gmax[:, :].unsqueeze(2).to_broadcast([128, TT, NE]),
                                            ALU.subtract).then_inc(s_glm, 1)

            def gates(b):
                dve.wait_ge(s_gle, b + 1)
                own(nc.vector.tensor_reduce(gden[:, :], gl[:, :, :], AX, ALU.add))
                own(nc.vector.reciprocal(gden[:, :], gden[:, :]))
                nc.vector.tensor_tensor(gate[:, :, :], gl[:, :, :], gden[:, :].unsqueeze(2).to_broadcast([128, TT, NE]),
                                        ALU.mult).then_inc(s_gate, 1)

            def sum_logits(t, hh):
                pr = prod[:, t, 1024 * hh:1024 * hh + 1024].rearrange("p (h g d) -> p h g d", h=G // 2, g=G)
                return nc.vector.tensor_reduce(att[:, t, 8 * hh:8 * hh + 8, :], pr, AX, ALU.add)

            def less_maximum(t):
                own(nc.vector.tensor_reduce(amax[:, t, :], att[:, t, :, :], AX, ALU.max))
                nc.vector.tensor_tensor(att[:, t, :, :], att[:, t, :, :],
                                        amax[:, t, :].unsqueeze(2).to_broadcast([128, G, G]),
                                        ALU.subtract).then_inc(s_attm, 1)

            def weight_sums(b, t):
                dve.wait_ge(s_atte, TT * b + t + 1)
                own(nc.vector.tensor_reduce(aden[:, t, :], att[:, t, :, :], AX, ALU.add))
                own(nc.vector.reciprocal(aden[:, t, :], aden[:, t, :]))

            def reduce_outputs(t):
                o_t = o2[:, t, :].rearrange("p (h d) -> p h d", h=G)
                for hh in range(2):
                    pr = prod[:, t, 1024 * hh:1024 * hh + 1024].rearrange("p (h d g) -> p h d g", h=G // 2, d=GD)
                    last = nc.vector.tensor_reduce(o_t[:, 8 * hh:8 * hh + 8, :], pr, AX, ALU.add)
                own(last)
                return nc.vector.tensor_tensor(o_t, o_t, aden[:, t, :].unsqueeze(2).to_broadcast([128, G, GD]),
                                               ALU.mult)

            def layer_norm_statistics(b):
                dve.wait_ge(*taken("out_proj", b))
                statistics(f_mv, f_stat, [tokens(b)[:, t, :] for t in range(TT)]).then_inc(s_fstat, 1)

            def layer_norm(b):
                dve.wait_ge(s_rr1, b + 1)
                normalise(hn, tokens(b), f_mv, rr1, TT).then_inc(s_hn, 1)
                if b >= 2:
                    dve.wait_ge(s_x23, b - 1)
                dve.wait_ge(s_frstd, b + 1)
                normalise(xl[:, b % 2, :, :], tokens(b), f_mv, f_rstd, TT).then_inc(s_xl, 1)

            def root_norm(b):
                dve.wait_ge(s_rr2, b + 1)
                for t in range(TT):
                    last = nc.vector.tensor_scalar(hn2[:, t, :], xl[:, b % 2, t, :], rr2[:, t:t + 1], None, ALU.mult)
                last.then_inc(s_hn2, 1)

            def mix_experts(b):
                dve.wait_ge(s_x23, b + 1)
                dve.wait_ge(s_gate, b + 1)
                for i in range(NE):
                    for t in range(TT):
                        if i % 4 == 0:
                            dve.wait_ge(*made(f"moe{2 * t + i // 4}", b))
                        if i:
                            dve.wait_ge(s_mix, TT * (i - 1) + t + 1)
                        side = side_banks[SIDE[f"moe{2 * t + i // 4}", b][0]]
                        row = x_in[:, TT * b + t, :]
                        nc.vector.scalar_tensor_tensor(row, side[:, D * (i % 4):D * (i % 4) + D],
                                                       gate[:, t, i:i + 1], row, ALU.mult, ALU.add).then_inc(s_mix, 1)

            def second_layer(slot, when):
                for b in range(NB):
                    if stands("reciprocals", b, slot, when):
                        reciprocals(b)
                    if stands("statistics", b, slot, when):
                        layer_norm_statistics(b)
                    if stands("layer_norm", b, slot, when):
                        layer_norm(b)
                    if stands("products_0", b, slot, when):
                        dve.wait_ge(*taken("keyval2", b))
                        for hh in range(2):
                            last = products(nc.vector, 0, hh)
                        own(last)
                    if stands("sum_0a", b, slot, when):
                        sum_logits(0, 0)
                    if stands("sum_0b", b, slot, when):
                        own(sum_logits(0, 1))
                        less_maximum(0)
                    if stands("sum_1a", b, slot, when):
                        dve.wait_ge(s_prod, b + 1)
                        sum_logits(1, 0)
                    if stands("sum_1b", b, slot, when):
                        own(sum_logits(1, 1))
                        less_maximum(1)
                    if stands("weigh_0a", b, slot, when):
                        weight_sums(b, 0)
                        weighted_values(nc.vector, 0, 0)
                    if stands("weigh_0b", b, slot, when):
                        own(weighted_values(nc.vector, 0, 1))
                    if stands("weigh_sum_1", b, slot, when):
                        weight_sums(b, 1)
                    if stands("reduce_0", b, slot, when):
                        reduce_outputs(0)
                    if stands("reduce_1", b, slot, when):
                        dve.wait_ge(s_prod2, b + 1)
                        reduce_outputs(1).then_inc(s_o2, 1)
                    if stands("root_norm", b, slot, when):
                        root_norm(b)
                    if stands("gates", b, slot, when):
                        gates(b)
                if (slot, when) == (LAST_SLOT - 1, "end"):
                    mix_experts(NB - 1)

            ctx_statistics(0)
            dve.wait_ge(ld["trig"], 32)
            for r in range(4):
                nc.vector.tensor_copy(trig4[:, 0, :, r, :], cos_in[:, :, :]).then_inc(s_trig, 1)
            ctx_normalise(0)
            for r in range(4):
                nc.vector.tensor_scalar(trig4[:, 1, :, r, :], sin_in[:, :, :], -1.0 if r % 2 == 0 else 1.0,
                                        None, ALU.mult).then_inc(s_trig, 1)
            tokens_statistics(0)
            dve.wait_ge(s_wkhi, 1)
            split_lo(wkA[:, 1, :], wk_in, wkA[:, 0, :]).then_inc(s_wk, 1)
            split_ctxT(0)
            tokens_normalise(0)
            dve.wait_ge(s_wk, 1)
            for s in range(2):
                src = f(wkA[:, s, :]).rearrange("k (h t i) -> k h t i", t=2, i=HALF)
                dst = wkB[:, s, :].rearrange("k (h t i) -> k h t i", t=2, i=HALF)
                for t in range(2):
                    last = nc.vector.tensor_copy(dst[:, :, t, :], src[:, :, 1 - t, :])
            last.then_inc(s_wk, 1)
            dve.wait_ge(s_wqhi, 2)
            wq_v = wq_in.rearrange("k (h d) -> k h d", h=H)
            own(split_lo(wqD[:, 1, :, 0, :], wq_v, wqD[:, 0, :, 0, :]))
            nc.vector.tensor_copy(wqD[:, 1, :, 1, :], f(wqD[:, 1, :, 0, :])).then_inc(s_wq, 1)
            split_latT(0)

            for slot in range(-KV_AHEAD, LAST_SLOT):
                b, p = divmod(slot, PAIRS)
                more = 0 <= b < NB - 1
                if slot + KV_AHEAD < NPAIR:
                    key_products(slot + KV_AHEAD)
                if more and p == 5:
                    split_ctxT(b + 1)
                second_layer(slot, "first")
                if slot == 0:
                    dve.wait_ge(s_const, 3)
                    nc.vector.tensor_copy(spread[:, :, :], spread_f[:, :, :]).then_inc(s_spread, 1)
                if 0 <= slot < NPAIR:
                    clip(slot, 0)
                side_taken(slot, "a")
                second_layer(slot, "early")
                if 0 <= slot + 1 < NPAIR:
                    query_lo(slot + 1)
                if more and p == 6:
                    split_latT(b + 1)
                if 0 <= slot + 1 < NPAIR:
                    key_lo(slot + 1)
                second_layer(slot, "mid")
                if 0 <= slot < NPAIR:
                    clip(slot, 1)
                second_layer(slot, "late")
                side_taken(slot, "b")
                if more:
                    if p == 1:
                        ctx_statistics(b + 1)
                        tokens_statistics(b + 1)
                    if p == 2:
                        ctx_normalise(b + 1)
                        tokens_normalise(b + 1)
                if p == 2 and 1 <= b <= NB:
                    take("out_proj", b - 1)
                side_taken(slot, "c")
                second_layer(slot, "end")

        @block.gpsimd
        def _(pool):
            def own(ins):
                own.n += 1
                ins.then_inc(own_pool, 1)
                pool.wait_ge(own_pool, own.n)
            own.n = 0

            def inverse_root(dst, var, eps):
                own(nc.gpsimd.tensor_scalar_add(dst, var, eps))
                return nc.gpsimd.tensor_tensor(dst, dst, half_p[:, 0:dst.shape[1]], ALU.pow)

            def ctx_rstd(b):
                pool.wait_ge(s_cstat, b + 1)
                inverse_root(c_rstd[:, :], c_mv[:, :, 1], LN_EPS).then_inc(s_crstd, 1)

            def two_norms(dst, var, eps):
                own(nc.gpsimd.tensor_scalar(dst, var, 1.0 + eps, LN_EPS * eps, ALU.mult, ALU.add))
                return nc.gpsimd.tensor_tensor(dst, dst, half_p[:, 0:dst.shape[1]], ALU.pow)

            def tokens_rstd(b):
                pool.wait_ge(s_lstat, b + 1)
                two_norms(l_rstd[:, :], l_mv[:, :, 1], LN_EPS).then_inc(s_lrstd, 1)

            def mean_square_root(dst, ss):
                own(nc.gpsimd.tensor_scalar(dst[:, :], ss[:, :], 1.0 / D, RMS_EPS, ALU.mult, ALU.add))
                return nc.gpsimd.tensor_tensor(dst[:, :], dst[:, :], half_p[:, 0:TT], ALU.pow)

            nc.gpsimd.memset(half_p[:, :], -0.5)
            own(nc.gpsimd.memset(ident[:, :], 0.0))
            nc.gpsimd.affine_select(out=ident[:, :], in_=ident[:, :], compare_op=ALU.not_equal, fill=1.0, base=0,
                                    pattern=[[-1, 128]], channel_multiplier=1).then_inc(s_const, 1)
            own(nc.gpsimd.memset(sum_rows[:, :], 0.0))
            nc.gpsimd.memset(sum_rows[:, 24:32], 1.0).then_inc(s_const, 1)
            own(nc.gpsimd.memset(spread_f[:, :, :], 0.0))
            sp_v = spread_f[:, :, :].rearrange("k (i q) (h c) -> k i q h c", q=2, h=2)
            nc.gpsimd.affine_select(out=sp_v, in_=sp_v, compare_op=ALU.not_equal, fill=1.0, base=0,
                                    pattern=[[-8, PAIRS // 2], [-64, 2], [-32, 2], [0, DH]], channel_multiplier=1)\
                .then_inc(s_const, 1)
            ctx_rstd(0)
            tokens_rstd(0)
            pool.wait_ge(s_wvhi, 1)
            nc.gpsimd.tensor_tensor(wvS[:, 1, :], wv_in, f(wvS[:, 0, :]), ALU.subtract).then_inc(s_wv, 1)

            def rotate(j):
                pool.wait_ge(s_kmul, 2 * j + 2)
                if j >= 2:
                    pool.wait_ge(s_klo, 2 * (j - 1))
                nc.gpsimd.tensor_tensor(krot[:, j % 2, :], kcos[:, j % 2, :], ksin[:, j % 2, :], ALU.add)\
                    .then_inc(s_krot, 1)

            def chunk_sums(j, h):
                n = 2 * j + h
                pool.wait_ge(s_clip, n + 1)
                if j >= 2 and h == 0:
                    pool.wait_ge(s_sum, j // 2)
                nc.gpsimd.tensor_tensor(esum[:, n % 4, :, :], e[:, n % 4, 0:2, :], e[:, n % 4, 2:4, :], ALU.add)\
                    .then_inc(s_esum, 1)

            def sum_experts(b, t):
                pool.wait_ge(*taken(f"moe{2 * t + 1}", b))
                pool.wait_ge(s_moe, 6 * (TT * b + t + 1))
                n = NE
                while n > 1:
                    n //= 2
                    own(nc.gpsimd.tensor_tensor(moe[:, t, 0:n, :], moe[:, t, 0:n, :], moe[:, t, n:2 * n, :], ALU.add))
                nc.gpsimd.tensor_tensor(x_in[:, TT * b + t, :], x_in[:, TT * b + t, :], moe[:, t, 0, :], ALU.add)\
                    .then_inc(s_y, 1)

            def second_layer(slot, part):
                for b in range(NB):
                    if stands("add_bias", b, slot, part):
                        if b == 0:
                            pool.wait_ge(ld["bias"], 16 * 6)
                        pool.wait_ge(s_latn, b + 1)
                        tokens = x_in[:, TT * b:TT * b + TT, :]
                        nc.gpsimd.tensor_tensor(tokens, tokens, bo_r[:, :].unsqueeze(1).to_broadcast([128, TT, D]),
                                                ALU.add).then_inc(s_xb, 1)
                    if stands("two_norms", b, slot, part):
                        pool.wait_ge(s_fstat, b + 1)
                        two_norms(rr1[:, :], f_mv[:, :, 1], RMS_EPS).then_inc(s_rr1, 1)
                        inverse_root(f_rstd[:, :], f_mv[:, :, 1], LN_EPS).then_inc(s_frstd, 1)
                    if stands("xl_bias", b, slot, part):
                        pool.wait_ge(s_xl, b + 1)
                        nc.gpsimd.tensor_tensor(xl[:, b % 2, :, :], xl[:, b % 2, :, :],
                                                fbo_r[:, :].unsqueeze(1).to_broadcast([128, TT, D]), ALU.add)\
                            .then_inc(s_xlb, 1)
                    if stands("products_1a", b, slot, part):
                        pool.wait_ge(*taken("keyval2", b))
                        products(nc.gpsimd, 1, 0)
                    if stands("products_1b", b, slot, part):
                        products(nc.gpsimd, 1, 1).then_inc(s_prod, 1)
                    if stands("weigh_1a", b, slot, part):
                        pool.wait_ge(s_atte, TT * b + 2)
                        weighted_values(nc.gpsimd, 1, 0)
                    if stands("weigh_1b", b, slot, part):
                        weighted_values(nc.gpsimd, 1, 1).then_inc(s_prod2, 1)
                    if stands("mean_square", b, slot, part):
                        pool.wait_ge(s_ss2, b + 1)
                        mean_square_root(rr2, ss2).then_inc(s_rr2, 1)
                        tokens = x_in[:, TT * b:TT * b + TT, :]
                        nc.gpsimd.tensor_tensor(tokens, tokens, xl[:, b % 2, :, :], ALU.add).then_inc(s_x23, 1)
                    for t in range(TT):
                        if b < NB - 1 and stands(f"sum_experts_{t}", b, slot, part):
                            pool.wait_ge(s_x23, b + 1)
                            sum_experts(b, t)

            for slot in range(-KV_AHEAD, LAST_SLOT):
                b, p = divmod(slot, PAIRS)
                if slot + KV_AHEAD < NPAIR:
                    rotate(slot + KV_AHEAD)
                second_layer(slot, -1)
                if 0 <= slot < NPAIR - 2:
                    chunk_sums(slot, 0)
                second_layer(slot, 0)
                if 0 <= slot < NPAIR - 2:
                    chunk_sums(slot, 1)
                second_layer(slot, 1)
                if 0 <= b < NB - 1:
                    if p == 1:
                        ctx_rstd(b + 1)
                        tokens_rstd(b + 1)


_INS = ['x', 'ctx_1024', 'L0_xattn_cos', 'L0_xattn_sin', 'L0_xattn_ln_lat_g', 'L0_xattn_ln_lat_b',
        'L0_xattn_ln_ctx_g', 'L0_xattn_ln_ctx_b', 'L0_xattn_Wq', 'L0_xattn_Wkv', 'L0_xattn_Wo', 'L0_xattn_bo',
        'L0_ffn_gamma1', 'L0_ffn_Wq', 'L0_ffn_bq', 'L0_ffn_Wdown', 'L0_ffn_bdown', 'L0_ffn_Wup', 'L0_ffn_bup',
        'L0_ffn_Wo', 'L0_ffn_bo', 'L0_ffn_gamma2', 'L0_ffn_Wg', 'L0_ffn_bg', 'L0_ffn_We']
_OUTS = [((4, 256, 128), 'float32')]


def kernel(**inputs):
    import numpy as _np
    import concourse.bacc as _bacc
    from concourse import mybir as _mybir
    from concourse.bass_utils import run_bass_kernel_spmd as _run

    nc = _bacc.Bacc("TRN2", target_bir_lowering=False, num_devices=1)
    arrays, args = {}, []
    for name in _INS:
        a = _np.ascontiguousarray(inputs[name])
        arrays[f"in_{name}_dram"] = a
        args.append(nc.dram_tensor(f"in_{name}_dram", a.shape, _mybir.dt.from_np(a.dtype), kind="ExternalInput").ap())
    for i, (shape, dtype) in enumerate(_OUTS):
        dt = _mybir.dt.from_np(_np.dtype(dtype))
        args.append(nc.dram_tensor(f"out_{i}_dram", shape, dt, kind="ExternalOutput").ap())
    xattn_ffn(nc, *args)
    r = _run(nc, [arrays], core_ids=[0])
    got = tuple(r.results[0][f"out_{i}_dram"] for i in range(len(_OUTS)))
    return got[0]
```
